# Optimizing a Trainium2 kernel written in Bass

```python
import numpy as np
import jax
import jax.numpy as jnp

def _softmax(x, axis=-1):
    return jax.nn.softmax(x, axis=axis)

def _gelu(x):
    return jax.nn.gelu(x, approximate=True)

def _silu(x):
    return jax.nn.silu(x)

def _sigmoid(x):
    return jax.nn.sigmoid(x)

def _layernorm(x, axis=-1, eps=1e-05):
    m = jnp.mean(x, axis=axis, keepdims=True)
    v = jnp.var(x, axis=axis, keepdims=True)
    return (x - m) / jnp.sqrt(v + eps)

def _scatter_add(tgt, idx, src, axis=0):
    return tgt.at[idx].add(src)

def _segment_sum(src, seg, n):
    return jax.ops.segment_sum(src, seg, n)
kernel_name = 'mk_xattn_seq_d1_seqx_r2_5455ae'

def setup_inputs(seed: int=0):
    np.random.seed(seed)
    _w = jnp.asarray

    def _rec_inputs():
        import jax
        import jax.numpy as jnp
        _rk = jax.random.key(seed)
        x = 7.22e-05 + 1 * jax.random.normal(jax.random.fold_in(_rk, 1), (32, 512, 512), jnp.float32)
        _lenS = 512 - jax.random.randint(jax.random.fold_in(_rk, 7), (32,), 0, max(1, 512 // 4) + 1, jnp.int32)
        _lenS2 = 77 - jax.random.randint(jax.random.fold_in(_rk, 8), (32,), 0, max(1, 77 // 4) + 1, jnp.int32)
        _ctx_1024P = jax.random.normal(jax.random.fold_in(_rk, 11), (32, 16, 512), jnp.float32)
        _ctx_1024c = jax.random.dirichlet(jax.random.fold_in(_rk, 511), 0.3 * jnp.ones((16,), jnp.float32), (32, 77))
        _ctx_1024t = jnp.einsum('bsk,bkd->bsd', _ctx_1024c, _ctx_1024P)
        _ctx_1024t = _ctx_1024t * jax.lax.rsqrt(jnp.mean(jnp.square(_ctx_1024t)) + 1e-12) * 0.953939
        ctx_1024 = 4.13588e-05 + 0.999923 * (_ctx_1024t + 0.3 * jax.random.normal(jax.random.fold_in(_rk, 611), (32, 77, 512), jnp.float32))
        return (x, ctx_1024)
    x, ctx_1024 = _rec_inputs()

    def _L0_xattn_setup():
        import jax, jax.numpy as jnp
        import numpy as np
        D_MODEL, D_ATT, N_HEADS = (512, 64, 16)
        EPS = 1e-05

        def layernorm(x, gamma, beta):
            mu = jnp.mean(x, axis=-1, keepdims=True)
            var = jnp.mean((x - mu) ** 2, axis=-1, keepdims=True)
            return gamma * (x - mu) * jax.lax.rsqrt(var + EPS) + beta
        key = jax.random.key(seed)
        ks = jax.random.split(key, 12)
        B, S = (4, 1024)
        H = N_HEADS * D_ATT
        sd = 1.0 / np.sqrt(D_MODEL)
        return {'state': jax.random.normal(ks[0], (B, S, D_MODEL), jnp.float32), 'context': jax.random.normal(ks[1], (B, S, D_MODEL), jnp.float32), 'Wq': jax.random.normal(ks[2], (D_MODEL, H), jnp.float32) * sd, 'bq': jnp.zeros((H,), jnp.float32), 'Wk': jax.random.normal(ks[3], (D_MODEL, H), jnp.float32) * sd, 'bk': jnp.zeros((H,), jnp.float32), 'Wv': jax.random.normal(ks[4], (D_MODEL, H), jnp.float32) * sd, 'bv': jnp.zeros((H,), jnp.float32), 'Wo': jax.random.normal(ks[5], (H, D_MODEL), jnp.float32) * sd, 'bo': jnp.zeros((D_MODEL,), jnp.float32), 'ln_gamma': jnp.ones((D_MODEL,), jnp.float32), 'ln_beta': jnp.zeros((D_MODEL,), jnp.float32)}
    _L0_xattn_all = _L0_xattn_setup()
    _L0_xattn_in = {k: v for k, v in _L0_xattn_all.items() if k in ('Wq', 'bq', 'Wk', 'bk', 'Wv', 'bv', 'Wo', 'bo', 'ln_gamma', 'ln_beta')}
    del _L0_xattn_all
    return {'x': x, 'ctx_1024': ctx_1024, 'L0_xattn_Wq': _L0_xattn_in['Wq'], 'L0_xattn_bq': _L0_xattn_in['bq'], 'L0_xattn_Wk': _L0_xattn_in['Wk'], 'L0_xattn_bk': _L0_xattn_in['bk'], 'L0_xattn_Wv': _L0_xattn_in['Wv'], 'L0_xattn_bv': _L0_xattn_in['bv'], 'L0_xattn_Wo': _L0_xattn_in['Wo'], 'L0_xattn_bo': _L0_xattn_in['bo'], 'L0_xattn_ln_gamma': _L0_xattn_in['ln_gamma'], 'L0_xattn_ln_beta': _L0_xattn_in['ln_beta']}

def reference(x, ctx_1024, L0_xattn_Wq, L0_xattn_bq, L0_xattn_Wk, L0_xattn_bk, L0_xattn_Wv, L0_xattn_bv, L0_xattn_Wo, L0_xattn_bo, L0_xattn_ln_gamma, L0_xattn_ln_beta):
    import jax
    import jax.numpy as jnp

    def _L0_xattn_ref(state, context, Wq, bq, Wk, bk, Wv, bv, Wo, bo, ln_gamma, ln_beta):
        import jax, jax.numpy as jnp
        import numpy as np
        D_MODEL, D_ATT, N_HEADS = (512, 64, 16)
        EPS = 1e-05

        def layernorm(x, gamma, beta):
            mu = jnp.mean(x, axis=-1, keepdims=True)
            var = jnp.mean((x - mu) ** 2, axis=-1, keepdims=True)
            return gamma * (x - mu) * jax.lax.rsqrt(var + EPS) + beta
        B, S, _ = state.shape
        xs = layernorm(state, ln_gamma, ln_beta)
        xc = layernorm(context, ln_gamma, ln_beta)

        def split_heads(x):
            return x.reshape(B, -1, N_HEADS, D_ATT).transpose(0, 2, 1, 3)
        q = split_heads(xs @ Wq + bq)
        k = split_heads(xc @ Wk + bk)
        v = split_heads(xc @ Wv + bv)
        scale = 1.0 / jnp.sqrt(jnp.asarray(D_ATT, q.dtype))
        scores = jnp.einsum('bhqd,bhkd->bhqk', q, k) * scale
        attn = jax.nn.softmax(scores, axis=-1)
        o = jnp.einsum('bhqk,bhkd->bhqd', attn, v)
        o = o.transpose(0, 2, 1, 3).reshape(B, S, N_HEADS * D_ATT)
        out = o @ Wo + bo
        return out + state
    x = _L0_xattn_ref(x, ctx_1024, L0_xattn_Wq, L0_xattn_bq, L0_xattn_Wk, L0_xattn_bk, L0_xattn_Wv, L0_xattn_bv, L0_xattn_Wo, L0_xattn_bo, L0_xattn_ln_gamma, L0_xattn_ln_beta)
    return x

_drawn_inputs = setup_inputs


def setup_inputs(seed=0):
    import zlib

    import numpy as np

    out = dict(_drawn_inputs(seed))
    spreads = {'L0_xattn_bq': (0.0, 0.339),
     'L0_xattn_bk': (0.0, 0.8),
     'L0_xattn_bv': (0.0, 0.1),
     'L0_xattn_bo': (0.0, 0.1),
     'L0_xattn_ln_gamma': (1.0, 0.2),
     'L0_xattn_ln_beta': (0.0, 0.1)}
    factors = {}
    for name, (base, spread) in spreads.items():
        noise = np.random.default_rng([zlib.crc32(name.encode()), seed]).standard_normal(out[name].shape)
        drawn = base * np.exp(spread * noise) if base else spread * noise
        out[name] = jnp.asarray(drawn.astype(out[name].dtype))
    for name, factor in factors.items():
        out[name] = (out[name] * factor).astype(out[name].dtype)
    return out
```

```python
from contextlib import ExitStack

import concourse.bass as bass
from concourse import mybir

F32 = mybir.dt.float32
F32R = mybir.dt.float32r
ALU = mybir.AluOpType
ACT = mybir.ActivationFunctionType
AX_X = mybir.AxisListType.X

P = 128
EPS = 1e-5


def three_passes(nc, out, stationary, moving, first, last):
    (s_hi, s_lo), (m_hi, m_lo) = stationary, moving
    nc.tensor.matmul(out, s_hi, m_hi, start=first, stop=False)
    nc.tensor.matmul(out, s_hi, m_lo, start=False, stop=False)
    return nc.tensor.matmul(out, s_lo, m_hi, start=False, stop=last)


def offset(eng, value):
    return value if type(value) is int else eng.snap(value)


def build_kernel(nc, x, ctx_in, wq, bq, wk, bk, wv, bv, wo, bo, gamma, beta, out):
    B, S, D = x.shape
    KEYS = ctx_in.shape[1]
    H = wq.shape[1]
    DH = 64
    PAIRS = H // P
    DC = D // P
    QT = S // P
    ROWS = B * KEYS
    GROUP = 512
    GROUPS = -(-ROWS // GROUP)
    STEP = (ROWS - GROUP) // (GROUPS - 1)
    assert STEP * (GROUPS - 1) + GROUP == ROWS and STEP <= GROUP
    RT = GROUP // P
    HALF = H // 2
    W2 = 2 * KEYS
    K_SCALE = float(DH) ** -0.5
    assert K_SCALE == 0.125 and D == 512 and S == 512 and H == 1024

    k_dram = nc.dram_tensor("k_scratch", (PAIRS, P, ROWS), F32, kind="Internal").ap()
    v_dram = nc.dram_tensor("v_scratch", (ROWS, H), F32, kind="Internal").ap()
    ctx_rows = ctx_in.rearrange("b s d -> (b s) d")

    with ExitStack() as whole:
        def sem(name):
            return whole.enter_context(nc.semaphore(name))

        def sb(stack, name, shape, dt=F32):
            return stack.enter_context(nc.sbuf_tensor(name, shape, dt))

        banks = [whole.enter_context(nc.psum_tensor(f"bank{i}", [P, 512], F32)) for i in range(8)]

        wq_s = sb(whole, "wq_s", [P, 2, DC, H], F32R)
        wo_s = sb(whole, "wo_s", [P, 2, PAIRS, D], F32R)
        ident = sb(whole, "ident", [P, P])
        gam = sb(whole, "gam", [P, DC])
        bet = sb(whole, "bet", [P, DC])
        bq_c = sb(whole, "bq_c", [P, PAIRS])
        minus_half = sb(whole, "minus_half", [P, 4])
        eps_c = sb(whole, "eps_c", [P, 4])

        project_context(nc, sem, sb, banks, locals())
        attend(nc, sem, sb, banks, locals())


def project_context(nc, sem, sb, banks, g):
    B, D, H, PAIRS, DC, ROWS = g["B"], g["D"], g["H"], g["PAIRS"], g["DC"], g["ROWS"]
    GROUP, GROUPS, STEP, RT, K_SCALE = g["GROUP"], g["GROUPS"], g["STEP"], g["RT"], g["K_SCALE"]
    HALF = g["HALF"]
    wq_s, wo_s, ident, gam, bet, bq_c, minus_half, eps_c = (
        g["wq_s"], g["wo_s"], g["ident"], g["gam"], g["bet"], g["bq_c"], g["minus_half"], g["eps_c"])
    wq, wk, wv, wo, bq, bk, bv = g["wq"], g["wk"], g["wv"], g["wo"], g["bq"], g["bk"], g["bv"]
    k_dram, v_dram, ctx_rows = g["k_dram"], g["v_dram"], g["ctx_rows"]

    with ExitStack() as st:
        wk_s = sb(st, "wk_s", [P, 2, DC, H], F32R)
        wv_s = sb(st, "wv_s", [P, 2, DC, H], F32R)
        w_raw = sb(st, "w_raw", [P, 2, H])
        c_n = sb(st, "c_n", [P, RT, D])
        c_T = sb(st, "c_T", [P, 2, DC, P])
        c_s = sb(st, "c_s", [P, 2, DC, GROUP], F32R)
        k_st = sb(st, "k_st", [P, 2, GROUP])
        v_st = sb(st, "v_st", [P, 2, H])
        bv_b = sb(st, "bv_b", [P, H])
        bk_c = sb(st, "bk_c", [P, PAIRS])
        bk_8 = sb(st, "bk_8", [P, PAIRS])
        stats = sb(st, "c_stats", [P, RT, 6])
        mv = sb(st, "c_mv", [P, RT, 2])
        counts = sb(st, "c_counts", [P, 1])
        var_eps = sb(st, "c_var_eps", [P, RT])
        rstd = sb(st, "c_rstd", [P, RT])
        ps_k = [banks[0], banks[1]]
        ps_v = [[banks[2], banks[3]], [banks[4], banks[5]]]
        ps_t = [banks[6], banks[7]]

        consts_loaded = sem("consts_loaded")
        bv_loaded = sem("bv_loaded")
        ctx_loaded = [sem(f"ctx_loaded{t}") for t in range(RT)]
        w_loaded = [sem("w_loaded0"), sem("w_loaded1")]
        consts_made = sem("consts_made")
        w_rounded = sem("w_rounded")
        w_split = sem("w_split")
        bk_scaled = sem("bk_scaled")
        c_stats_done = sem("c_stats_done")
        c_aggregated = sem("c_aggregated")
        c_var_eps = sem("c_var_eps")
        c_counted = sem("c_counted")
        c_rstd_done = sem("c_rstd_done")
        c_normed = sem("c_normed")
        c_transposed = sem("c_transposed")
        cT_ready = sem("cT_ready")
        c_rounded = sem("c_rounded")
        c_split = sem("c_split")
        k_projected = sem("k_projected")
        k_ready = sem("k_ready")
        k_stored = [sem("k_stored0"), sem("k_stored1")]
        v_projected = sem("v_projected")
        v_ready = sem("v_ready")
        v_stored = [sem("v_stored0"), sem("v_stored1")]

        chunks = [(w.rearrange("(c p) n -> c p n", p=P)[c], [ws[:, i, c, :] for i in range(2)])
                  for w, ws in ((wk, wk_s), (wv, wv_s), (wq, wq_s)) for c in range(DC)]
        chunks += [(wo.rearrange("(c a p) n -> c p a n", p=P, a=2)[c],
                    [wo_s[:, i, 2 * c:2 * c + 2, :] for i in range(2)]) for c in range(PAIRS // 2)]
        EARLY = 2 * DC

        block = st.enter_context(nc.Block())

        @block.sync
        def _(sp):
            def load_context(row, t):
                sp.dma_start(c_n[:, t, :], ctx_rows[bass.ds(row, P), :]).then_inc(ctx_loaded[t], 16)

            def load_weight(n):
                if n >= 2:
                    sp.wait_ge(w_split, n - 1)
                dst = w_raw[:, n % 2, :]
                if n >= 3 * DC:
                    dst = dst.rearrange("p (a n) -> p a n", a=2)
                sp.dma_start(dst, chunks[n][0]).then_inc(w_loaded[n % 2], 16)

            load_context(0, 0)
            for dst, src in ((gam, g["gamma"]), (bet, g["beta"]), (bq_c, bq), (bk_c, bk)):
                sp.dma_start(dst[:, :], src).then_inc(consts_loaded, 16)
            load_weight(0)
            load_context(P, 1)
            load_weight(1)
            for t in range(2, RT):
                load_context(t * P, t)
            for n in range(2, EARLY):
                load_weight(n)
            sp.dma_start(bv_b[:, :], bv.rearrange("(a n) -> a n", a=1).to_broadcast([P, H])).then_inc(bv_loaded, 16)

            def group(r, first, last):
                if not last:
                    next_rows = [offset(sp, r * STEP + STEP + t * P) for t in range(RT)]
                    for t in range(RT):
                        sp.wait_ge(c_transposed, RT * r + t + 1)
                        load_context(next_rows[t], t)
                if first:
                    for n in range(EARLY, len(chunks)):
                        load_weight(n)

            group(0, True, False)
            with sp.Fori(1, GROUPS - 1) as r:
                group(r, False, False)
            for s in range(2):
                sp.wait_ge(k_stored[s], 16 * (PAIRS // 2) * GROUPS)
                sp.wait_ge(v_stored[s], 16 * (RT // 2) * GROUPS)

        @block.gpsimd
        def _(pool):
            pool.memset(ident[:, :], 0.0).then_inc(consts_made, 1)
            pool.memset(minus_half[:, :], -0.5).then_inc(consts_made, 1)
            pool.memset(eps_c[:, :], EPS).then_inc(consts_made, 1)
            pool.wait_ge(consts_made, 3)
            pool.affine_select(out=ident[:, :], in_=ident[:, :], compare_op=ALU.not_equal, fill=1.0, base=0,
                               pattern=[[-1, P]], channel_multiplier=1).then_inc(consts_made, 1)

            def rstd_of(r):
                pool.wait_ge(c_aggregated, RT * (r + 1))
                pool.tensor_tensor(var_eps[:, :], mv[:, :, 1], eps_c[:, 0:RT], ALU.add).then_inc(c_var_eps, 1)
                pool.wait_ge(c_var_eps, r + 1)
                pool.tensor_tensor(rstd[:, :], var_eps[:, :], minus_half[:, 0:RT], ALU.pow).then_inc(c_rstd_done, 1)

            rstd_of(0)
            with pool.Fori(1, GROUPS) as r:
                rstd_of(r)

        @block.vector
        def _(dve):
            def statistics(r):
                for t in range(RT):
                    dve.wait_ge(ctx_loaded[t], 16 * (r + 1))
                    nc.vector.bn_stats(stats[:, t, :], c_n[:, t, :]).then_inc(c_stats_done, 1)
                dve.wait_ge(c_stats_done, RT * (r + 1))
                nc.vector.tensor_copy(counts[:, :], stats[:, RT - 1, 0:1]).then_inc(c_counted, 1)
                for t in range(RT):
                    nc.vector.bn_aggr(mv[:, t, :], stats[:, t, :]).then_inc(c_aggregated, 1)

            def normalise(r):
                for t in range(RT):
                    dve.wait_ge(c_rstd_done, r + 1)
                    nc.vector.tensor_scalar(c_n[:, t, :], c_n[:, t, :], mv[:, t, 0:1], rstd[:, t:t + 1],
                                            ALU.subtract, ALU.mult).then_inc(c_normed, 1)

            def split_weight(n):
                raw = w_raw[:, n % 2, :]
                if n >= 3 * DC:
                    raw = raw.rearrange("p (a n) -> p a n", a=2)
                hi, lo = chunks[n][1]
                dve.wait_ge(w_loaded[n % 2], 16 * (n // 2 + 1))
                nc.vector.tensor_copy(hi, raw).then_inc(w_rounded, 1)
                dve.wait_ge(w_rounded, n + 1)
                nc.vector.tensor_tensor(lo, raw, hi.bitcast(F32), ALU.subtract).then_inc(w_split, 1)

            def split_context(r, t):
                cols = slice(t * P, (t + 1) * P)
                dve.wait_ge(cT_ready, (RT * r + t + 1) * DC)
                nc.vector.tensor_copy(c_s[:, 0, :, cols], c_T[:, t % 2]).then_inc(c_rounded, 1)
                dve.wait_ge(c_rounded, RT * r + t + 1)
                nc.vector.tensor_tensor(c_s[:, 1, :, cols], c_T[:, t % 2], c_s[:, 0, :, cols].bitcast(F32),
                                        ALU.subtract).then_inc(c_split, 1)

            dve.wait_ge(consts_loaded, 64)
            nc.vector.tensor_scalar(bk_8[:, :], bk_c[:, :], K_SCALE, None, ALU.mult).then_inc(bk_scaled, 1)
            statistics(0)
            split_weight(0)
            normalise(0)
            split_weight(1)
            for t in range(RT):
                split_context(0, t)
                split_weight(2 + t)
            for n in range(2 + RT, EARLY):
                split_weight(n)
            dve.wait_ge(bv_loaded, 16)

            def group(r, first, last):
                if first:
                    for m in range(PAIRS):
                        split_weight(EARLY + m)
                if not last:
                    statistics(r + 1)
                    normalise(r + 1)
                for t in range(RT):
                    for n in range(2):
                        dve.wait_ge(v_projected, 2 * RT * r + 2 * t + n + 1)
                        if t >= 2:
                            dve.wait_ge(v_stored[t % 2], 16 * ((RT // 2) * r + 1))
                        elif not first:
                            dve.wait_ge(v_stored[t % 2], 16 * (RT // 2) * r)
                        nc.vector.tensor_tensor(v_st[:, t % 2, n * HALF:(n + 1) * HALF], ps_v[t % 2][n][:, :],
                                                bv_b[:, n * HALF:(n + 1) * HALF], ALU.add).then_inc(v_ready, 1)
                    if not last:
                        split_context(r + 1, t)

            group(0, True, False)
            with dve.Fori(1, GROUPS - 1) as r:
                group(r, False, False)
            group(GROUPS - 1, False, True)

        @block.scalar
        def _(act):
            def evacuate_transposed(r, t):
                act.wait_ge(c_transposed, RT * r + t + 1)
                for c in range(DC):
                    if c == 0:
                        if t >= 2:
                            act.wait_ge(c_split, RT * r + t - 1)
                        elif type(r) is not int or r > 0:
                            act.wait_ge(c_split, RT * r + t - 1)
                    nc.scalar.activation(c_T[:, t % 2, c, :], ps_t[t % 2][:, c * P:(c + 1) * P], ACT.Identity,
                                         bias=bet[:, c:c + 1], scale=gam[:, c:c + 1]).then_inc(cT_ready, 1)

            act.wait_ge(consts_loaded, 64)
            act.wait_ge(bk_scaled, 1)
            for t in range(RT):
                evacuate_transposed(0, t)

            def group(r, first, last):
                rows = [offset(act, r * STEP + t * P) for t in range(RT)]
                for m in range(PAIRS):
                    act.wait_ge(k_projected, PAIRS * r + m + 1)
                    if m >= 2:
                        act.wait_ge(k_stored[m % 2], 16 * ((PAIRS // 2) * r + m // 2))
                    elif not first:
                        act.wait_ge(k_stored[m % 2], 16 * (PAIRS // 2) * r)
                    nc.scalar.activation(k_st[:, m % 2, :], ps_k[m % 2][:, :], ACT.Identity,
                                         bias=bk_8[:, m:m + 1], scale=K_SCALE).then_inc(k_ready, 1)
                    act.wait_ge(k_ready, PAIRS * r + m + 1)
                    act.dma_start(k_dram[m, :, bass.ds(rows[0], GROUP)], k_st[:, m % 2, :]).then_inc(k_stored[m % 2], 16)
                for t in range(RT):
                    if not last:
                        evacuate_transposed(r + 1, t)
                    if t == 0 and not first:
                        act.wait_ge(v_stored[1], 16 * (RT // 2) * r)
                    act.wait_ge(v_ready, 2 * RT * r + 2 * t + 2)
                    act.dma_start(v_dram[bass.ds(rows[t], P), :], v_st[:, t % 2, :]).then_inc(v_stored[t % 2], 16)

            group(0, True, False)
            with act.Fori(1, GROUPS - 1) as r:
                group(r, False, False)
            group(GROUPS - 1, False, True)

        @block.tensor
        def _(pe):
            def transpose_tile(r, t, start):
                pe.wait_ge(c_normed, RT * r + t + 1)
                if not (start and t < 2):
                    pe.wait_ge(cT_ready, DC * (RT * r + t - 1))
                for c in range(DC):
                    last = nc.tensor.transpose(ps_t[t % 2][:, c * P:(c + 1) * P], c_n[:, t, c * P:(c + 1) * P],
                                               ident[:, :])
                last.then_inc(c_transposed, 1)

            pe.wait_ge(consts_made, 4)
            for t in range(RT):
                transpose_tile(0, t, True)

            def group(r, first, last):
                pe.wait_ge(c_split, RT * (r + 1))
                for m in range(PAIRS):
                    if m >= 2 or not first:
                        pe.wait_ge(k_ready, PAIRS * r + m - 1)
                    cols = slice(m * P, (m + 1) * P)
                    for c in range(DC):
                        if first and m == 0:
                            pe.wait_ge(w_split, c + 1)
                        mm = three_passes(nc, ps_k[m % 2][:, :], (wk_s[:, 0, c, cols], wk_s[:, 1, c, cols]),
                                          (c_s[:, 0, c, :], c_s[:, 1, c, :]), c == 0, c == DC - 1)
                    mm.then_inc(k_projected, 1)
                for t in range(RT):
                    rows = slice(t * P, (t + 1) * P)
                    for n in range(2):
                        cols = slice(n * HALF, (n + 1) * HALF)
                        if t >= 2 or not first:
                            pe.wait_ge(v_ready, 2 * RT * r + 2 * t + n - 3)
                        for c in range(DC):
                            if first and t == 0 and n == 0:
                                pe.wait_ge(w_split, DC + c + 1)
                            mm = three_passes(nc, ps_v[t % 2][n][:, :], (c_s[:, 0, c, rows], c_s[:, 1, c, rows]),
                                              (wv_s[:, 0, c, cols], wv_s[:, 1, c, cols]), c == 0, c == DC - 1)
                        mm.then_inc(v_projected, 1)
                    if not last:
                        transpose_tile(r + 1, t, False)

            group(0, True, False)
            with pe.Fori(1, GROUPS - 1) as r:
                group(r, False, False)
            group(GROUPS - 1, False, True)


def attend(nc, sem, sb, banks, g):
    B, S, D, KEYS, H = g["B"], g["S"], g["D"], g["KEYS"], g["H"]
    DH, PAIRS, DC, QT, W2 = g["DH"], g["PAIRS"], g["DC"], g["QT"], g["W2"]
    wq_s, wo_s, ident, gam, bet, bq_c, minus_half, eps_c = (
        g["wq_s"], g["wo_s"], g["ident"], g["gam"], g["bet"], g["bq_c"], g["minus_half"], g["eps_c"])
    x, bo, out, k_dram, v_dram = g["x"], g["bo"], g["out"], g["k_dram"], g["v_dram"]

    x_rows = x.rearrange("b s d -> (b s) d")
    out_rows = out.rearrange("b s d -> (b s) d")
    PV = 3 * DH

    with ExitStack() as st:
        x_in = sb(st, "x_in", [P, QT, D])
        x_bo = sb(st, "x_bo", [P, QT, D])
        x_n = sb(st, "x_n", [P, QT, D])
        x_T = sb(st, "x_T", [P, 2, S])
        x_s = sb(st, "x_s", [P, 2, DC, S], F32R)
        q_s = sb(st, "q_s", [P, 2, 2, S], F32R)
        k_in = sb(st, "k_in", [P, PAIRS, KEYS])
        k_s = sb(st, "k_s", [P, 2, PAIRS, W2], F32R)
        v_in = sb(st, "v_in", [KEYS, PAIRS, 2, DH])
        v_s = sb(st, "v_s", [KEYS, 2, PAIRS, PV], F32R)
        prob = sb(st, "prob", [P, 2, QT, 2, KEYS])
        pT_s = sb(st, "pT_s", [KEYS, 2, 2, 2, S], F32R)
        o_s = sb(st, "o_s", [P, 2, PAIRS, S], F32R)
        o_out = sb(st, "o_out", [P, 2, D])
        bo_b = sb(st, "bo_b", [P, D])
        neg_max = sb(st, "neg_max", [P, 2, QT, 2])
        sums = sb(st, "sums", [P, 2, QT, 2])
        recip = sb(st, "recip", [P, 2, QT, 2])
        stats = sb(st, "x_stats", [P, QT, 6])
        mv = sb(st, "x_mv", [P, QT, 2])
        counts = sb(st, "x_counts", [P, 1])
        var_eps = sb(st, "x_var_eps", [P, QT])
        rstd = sb(st, "x_rstd", [P, QT])
        v_halves = [v_s[:, i].rearrange("k m (a d) -> k m a d", a=3)[:, :, 0:3:2, :] for i in range(2)]
        ps_proj = [banks[0], banks[1]]
        ps_s = [banks[2], banks[3]]
        ps_pT = [banks[4], banks[5]]
        ps_o = [banks[6], banks[7]]

        bo_loaded = sem("bo_loaded")
        x_loaded = sem("x_loaded")
        k_loaded = sem("k_loaded")
        v_loaded = sem("v_loaded")
        zeroed = sem("zeroed")
        x_stats_done = sem("x_stats_done")
        x_aggregated = sem("x_aggregated")
        x_var_eps = sem("x_var_eps")
        x_counted = sem("x_counted")
        x_rstd_done = sem("x_rstd_done")
        x_normed = sem("x_normed")
        residual_ready = sem("residual_ready")
        x_transposed = sem("x_transposed")
        xT_ready = sem("xT_ready")
        x_rounded = sem("x_rounded")
        x_split = sem("x_split")
        kb_rounded = sem("kb_rounded")
        kb_split = sem("kb_split")
        vb_rounded = sem("vb_rounded")
        vb_split = sem("vb_split")
        q_projected = sem("q_projected")
        q_hi = sem("q_hi")
        q_lo = sem("q_lo")
        scores_ready = sem("scores_ready")
        max_ready = sem("max_ready")
        exp_ready = sem("exp_ready")
        recip_ready = sem("recip_ready")
        probs_ready = sem("probs_ready")
        probs_transposed = sem("probs_transposed")
        pT_hi = sem("pT_hi")
        pT_lo = sem("pT_lo")
        o_ready = sem("o_ready")
        o_hi = sem("o_hi")
        o_lo = sem("o_lo")
        out_projected = sem("out_projected")
        out_ready = sem("out_ready")
        out_stored = [sem("out_stored0"), sem("out_stored1")]

        Q_BANK = [0, 1, 0, 1, 0, 1, 0, 1]
        OUT_BANK = [1, 0, 1, 0]

        block = st.enter_context(nc.Block())


        @block.sync
        def _(sp):
            def load_x(row):
                sp.dma_start(x_in[:, :, :], x_rows[bass.ds(row, S), :].rearrange("(t p) d -> p t d", p=P)).then_inc(x_loaded, 16)

            def load_k(key):
                sp.dma_start(k_in[:, :, :], k_dram[:, :, bass.ds(key, KEYS)].rearrange("m p c -> p m c")).then_inc(k_loaded, 16)

            def load_v(key):
                sp.dma_start(v_in[:, :, :, :], v_dram[bass.ds(key, KEYS), :].rearrange("k (m a d) -> k m a d", m=PAIRS, a=2)).then_inc(v_loaded, 16)

            def store_out(b, rows):
                for t in range(QT):
                    sp.wait_ge(out_ready, QT * b + t + 1)
                    sp.dma_start(out_rows[bass.ds(rows[t], P), :], o_out[:, t % 2, :]).then_inc(out_stored[t % 2], 16)

            load_x(0)
            sp.dma_start(bo_b[:, :], bo.rearrange("(a n) -> a n", a=1).to_broadcast([P, D])).then_inc(bo_loaded, 16)
            load_k(0)
            load_v(0)

            def batch(b, first, last):
                if not last:
                    next_row, next_key = offset(sp, b * S + S), offset(sp, b * KEYS + KEYS)
                if not first:
                    out_row = [offset(sp, b * S + (t * P - S)) for t in range(QT)]
                if not last:
                    sp.wait_ge(kb_split, 2 * b + 2)
                    load_k(next_key)
                    sp.wait_ge(vb_split, b + 1)
                    load_v(next_key)
                if not first:
                    store_out(b - 1, out_row)
                if not last:
                    sp.wait_ge(residual_ready, QT * (b + 1))
                    load_x(next_row)

            batch(0, True, False)
            with sp.Fori(1, B - 1) as b:
                batch(b, False, False)
            batch(B - 1, False, True)
            store_out(B - 1, [(B - 1) * S + t * P for t in range(QT)])
            for s in range(2):
                sp.wait_ge(out_stored[s], 16 * (QT // 2) * B)

        @block.gpsimd
        def _(pool):
            pool.memset(k_s[:, :, :, :].bitcast(F32), 0.0).then_inc(zeroed, 1)
            pool.memset(v_s[:, :, :, :].bitcast(F32), 0.0).then_inc(zeroed, 1)
            pool.wait_ge(zeroed, 2)

            def rstd_of(b):
                pool.wait_ge(x_aggregated, QT * (b + 1))
                pool.tensor_tensor(var_eps[:, :], mv[:, :, 1], eps_c[:, 0:QT], ALU.add).then_inc(x_var_eps, 1)
                pool.wait_ge(x_var_eps, b + 1)
                pool.tensor_tensor(rstd[:, :], var_eps[:, :], minus_half[:, 0:QT], ALU.pow).then_inc(x_rstd_done, 1)

            def residual(b, first):
                for t in range(QT):
                    if not first:
                        pool.wait_ge(out_ready, QT * (b - 1) + t + 1)
                    pool.tensor_tensor(x_bo[:, t, :], x_in[:, t, :], bo_b[:, :], ALU.add).then_inc(residual_ready, 1)

            def values_low(b):
                pool.wait_ge(vb_rounded, b + 1)
                pool.tensor_tensor(v_halves[1], v_in[:, :, :, :], v_halves[0].bitcast(F32), ALU.subtract).then_inc(vb_split, 1)

            def divide(b, p):
                for h in range(2):
                    pr = prob[:, p % 2, 2 * h:2 * h + 2].rearrange("p t a k -> p (t a) k")
                    rc = recip[:, p % 2, 2 * h:2 * h + 2].rearrange("p t a -> p (t a)")
                    pool.wait_ge(recip_ready, 2 * (PAIRS * b + p) + h + 1)
                    pool.tensor_tensor(pr, pr, rc[:, :, None].to_broadcast([P, 4, KEYS]), ALU.mult).then_inc(probs_ready, 1)

            rstd_of(0)
            pool.wait_ge(bo_loaded, 16)

            def batch(b, first, last):
                divide(b, 0)
                values_low(b)
                divide(b, 1)
                residual(b, first)
                divide(b, 2)
                divide(b, 3)
                divide(b, 4)
                if not last:
                    rstd_of(b + 1)
                for p in range(5, PAIRS):
                    divide(b, p)

            batch(0, True, False)
            with pool.Fori(1, B - 1) as b:
                batch(b, False, False)
            batch(B - 1, False, True)

        @block.vector
        def _(dve):
            def statistics(b, tiles):
                for t in tiles:
                    dve.wait_ge(x_loaded, 16 * (b + 1))
                    nc.vector.bn_stats(stats[:, t, :], x_in[:, t, :]).then_inc(x_stats_done, 1)

            def aggregate(b):
                dve.wait_ge(x_stats_done, QT * (b + 1))
                nc.vector.tensor_copy(counts[:, :], stats[:, QT - 1, 0:1]).then_inc(x_counted, 1)
                for t in range(QT):
                    nc.vector.bn_aggr(mv[:, t, :], stats[:, t, :]).then_inc(x_aggregated, 1)

            def normalise_x(b):
                for t in range(QT):
                    dve.wait_ge(x_rstd_done, b + 1)
                    nc.vector.tensor_scalar(x_n[:, t, :], x_in[:, t, :], mv[:, t, 0:1], rstd[:, t:t + 1],
                                            ALU.subtract, ALU.mult).then_inc(x_normed, 1)

            def values_high(b, first):
                dve.wait_ge(v_loaded, 16 * (b + 1))
                if not first:
                    dve.wait_ge(o_ready, PAIRS * b)
                nc.vector.tensor_copy(v_halves[0], v_in[:, :, :, :]).then_inc(vb_rounded, 1)

            def split_x(b):
                for c in range(DC):
                    dve.wait_ge(xT_ready, DC * b + c + 1)
                    nc.vector.tensor_copy(x_s[:, 0, c, :], x_T[:, c % 2, :]).then_inc(x_rounded, 1)
                    dve.wait_ge(x_rounded, DC * b + c + 1)
                    nc.vector.tensor_tensor(x_s[:, 1, c, :], x_T[:, c % 2, :], x_s[:, 0, c, :].bitcast(F32),
                                            ALU.subtract).then_inc(x_split, 1)

            def split_keys(b, first):
                dve.wait_ge(k_loaded, 16 * (b + 1))
                if not first:
                    dve.wait_ge(scores_ready, 2 * PAIRS * b)
                for a in range(2):
                    rows, cols = slice(a * DH, (a + 1) * DH), slice(a * KEYS, (a + 1) * KEYS)
                    nc.vector.tensor_copy(k_s[rows, 0, :, cols], k_in[rows]).then_inc(kb_rounded, 1)
                for a in range(2):
                    rows, cols = slice(a * DH, (a + 1) * DH), slice(a * KEYS, (a + 1) * KEYS)
                    dve.wait_ge(kb_rounded, 2 * b + a + 1)
                    nc.vector.tensor_tensor(k_s[rows, 1, :, cols], k_in[rows], k_s[rows, 0, :, cols].bitcast(F32),
                                            ALU.subtract).then_inc(kb_split, 1)

            def query_low(b, p):
                j = PAIRS * b + p
                dve.wait_ge(q_hi, j + 1)
                nc.vector.scalar_tensor_tensor(out=q_s[:, p % 2, 1, :], in0=ps_proj[Q_BANK[p]][:, :],
                                               scalar=bq_c[:, p:p + 1], in1=q_s[:, p % 2, 0, :].bitcast(F32),
                                               op0=ALU.add, op1=ALU.subtract).then_inc(q_lo, 1)

            def maxima(b, p):
                for h in range(2):
                    dve.wait_ge(scores_ready, 2 * (PAIRS * b + p) + h + 1)
                    nc.vector.tensor_reduce(neg_max[:, p % 2, 2 * h:2 * h + 2, :].rearrange("p t a -> p (t a)"),
                                            ps_s[h][:, 0:2 * W2].rearrange("p (t k) -> p t k", k=KEYS),
                                            AX_X, ALU.max, negate=True).then_inc(max_ready, 1)

            def reciprocals(b, p):
                for h in range(2):
                    dve.wait_ge(exp_ready, 2 * (PAIRS * b + p) + h + 1)
                    nc.vector.reciprocal(recip[:, p % 2, 2 * h:2 * h + 2, :], sums[:, p % 2, 2 * h:2 * h + 2, :]).then_inc(recip_ready, 1)

            def probs_low(b, p):
                for a in range(2):
                    dve.wait_ge(pT_hi, 2 * (PAIRS * b + p) + a + 1)
                    nc.vector.tensor_tensor(pT_s[:, p % 2, a, 1, :], ps_pT[a][0:KEYS, :],
                                            pT_s[:, p % 2, a, 0, :].bitcast(F32), ALU.subtract).then_inc(pT_lo, 1)

            def output_low(b, p):
                dve.wait_ge(o_hi, PAIRS * b + p + 1)
                nc.vector.tensor_tensor(o_s[:, 1, p, :], ps_o[p % 2][:, :], o_s[:, 0, p, :].bitcast(F32),
                                        ALU.subtract).then_inc(o_lo, 1)

            def add_residual(b, first):
                for t in range(QT):
                    dve.wait_ge(out_projected, QT * b + t + 1)
                    dve.wait_ge(residual_ready, QT * b + t + 1)
                    if t >= 2:
                        dve.wait_ge(out_stored[t % 2], 16 * ((QT // 2) * b + 1))
                    elif not first:
                        dve.wait_ge(out_stored[t % 2], 16 * (QT // 2) * b)
                    nc.vector.tensor_tensor(o_out[:, t % 2, :], ps_proj[OUT_BANK[t]][:, :], x_bo[:, t, :],
                                            ALU.add).then_inc(out_ready, 1)

            statistics(0, range(QT))
            aggregate(0)
            normalise_x(0)
            split_x(0)
            dve.wait_ge(zeroed, 2)

            def batch(b, first, last):
                split_keys(b, first)
                query_low(b, 0)
                if not first:
                    probs_low(b - 1, 6)
                query_low(b, 1)
                if not first:
                    probs_low(b - 1, 7)
                    output_low(b - 1, 6)
                maxima(b, 0)
                reciprocals(b, 0)
                query_low(b, 2)
                if not first:
                    output_low(b - 1, 7)
                values_high(b, first)
                maxima(b, 1)
                reciprocals(b, 1)
                probs_low(b, 0)
                if not first:
                    add_residual(b - 1, False)
                for p in range(3, PAIRS):
                    query_low(b, p)
                    if p == 7 and not last:
                        split_x(b + 1)
                    maxima(b, p - 1)
                    reciprocals(b, p - 1)
                    probs_low(b, p - 2)
                    output_low(b, p - 3)
                    if p == 6 and not last:
                        normalise_x(b + 1)
                    if p == 4 and not last:
                        statistics(b + 1, range(0, 2))
                    if p == 5 and not last:
                        statistics(b + 1, range(2, QT))
                        aggregate(b + 1)
                maxima(b, 7)
                reciprocals(b, 7)
                output_low(b, 5)

            batch(0, True, False)
            with dve.Fori(1, B - 1) as b:
                batch(b, False, False)
            batch(B - 1, False, True)
            probs_low(B - 1, 6)
            probs_low(B - 1, 7)
            output_low(B - 1, 6)
            output_low(B - 1, 7)
            add_residual(B - 1, False)

        @block.scalar
        def _(act):
            def scale_x(b, first):
                for c in range(DC):
                    act.wait_ge(x_transposed, DC * b + c + 1)
                    if not (first and c < 2):
                        act.wait_ge(x_split, DC * b + c - 1)
                    nc.scalar.activation(x_T[:, c % 2, :], ps_proj[c % 2][:, :], ACT.Identity,
                                         bias=bet[:, c:c + 1], scale=gam[:, c:c + 1]).then_inc(xT_ready, 1)

            def query_high(b, p, first):
                j = PAIRS * b + p
                act.wait_ge(q_projected, j + 1)
                if not (first and p < 2):
                    act.wait_ge(scores_ready, 2 * j - 2)
                nc.scalar.activation(q_s[:, p % 2, 0, :], ps_proj[Q_BANK[p]][:, :], ACT.Identity,
                                     bias=bq_c[:, p:p + 1]).then_inc(q_hi, 1)

            def exponentials(b, p, first):
                j = PAIRS * b + p
                if not (first and p < 2):
                    act.wait_ge(probs_transposed, 2 * j - 2)
                for h in range(2):
                    act.wait_ge(max_ready, 2 * j + h + 1)
                    for n in range(4):
                        t, a = 2 * h + n // 2, n % 2
                        last = nc.scalar.activation(prob[:, p % 2, t, a, :], ps_s[h][:, n * KEYS:(n + 1) * KEYS], ACT.Exp,
                                                    bias=neg_max[:, p % 2, t, a:a + 1],
                                                    accum_out=sums[:, p % 2, t, a:a + 1])
                    last.then_inc(exp_ready, 1)

            def probs_high(b, p, first):
                j = PAIRS * b + p
                for a in range(2):
                    act.wait_ge(probs_transposed, 2 * j + a + 1)
                    if not (first and p < 2):
                        act.wait_ge(o_ready, j - 1)
                    nc.scalar.activation(pT_s[:, p % 2, a, 0, :], ps_pT[a][0:KEYS, :], ACT.Copy).then_inc(pT_hi, 1)

            def output_high(b, p, first):
                act.wait_ge(o_ready, PAIRS * b + p + 1)
                if not first:
                    act.wait_ge(out_projected, QT * b)
                nc.scalar.activation(o_s[:, 0, p, :], ps_o[p % 2][:, :], ACT.Copy).then_inc(o_hi, 1)

            scale_x(0, True)

            def batch(b, first, last):
                query_high(b, 0, first)
                if not first:
                    probs_high(b - 1, 6, False)
                query_high(b, 1, first)
                if not first:
                    probs_high(b - 1, 7, False)
                    output_high(b - 1, 6, True)
                exponentials(b, 0, first)
                query_high(b, 2, first)
                if not first:
                    output_high(b - 1, 7, True)
                exponentials(b, 1, first)
                probs_high(b, 0, first)
                for p in range(3, PAIRS):
                    query_high(b, p, first)
                    if p == 7 and not last:
                        scale_x(b + 1, False)
                    exponentials(b, p - 1, first)
                    probs_high(b, p - 2, first)
                    output_high(b, p - 3, first)
                exponentials(b, 7, first)
                output_high(b, 5, first)

            batch(0, True, False)
            with act.Fori(1, B - 1) as b:
                batch(b, False, False)
            batch(B - 1, False, True)
            probs_high(B - 1, 6, False)
            probs_high(B - 1, 7, False)
            output_high(B - 1, 6, True)
            output_high(B - 1, 7, True)

        @block.tensor
        def _(pe):
            def transpose_x(b, first):
                for c in range(DC):
                    if c == 0:
                        pe.wait_ge(x_normed, QT * (b + 1))
                    if c < 2 and not first:
                        pe.wait_ge(q_lo, PAIRS * b - 1 + c)
                    if c >= 2:
                        pe.wait_ge(xT_ready, DC * b + c - 1)
                    for t in range(QT):
                        last = nc.tensor.transpose(ps_proj[c % 2][:, t * P:(t + 1) * P],
                                                   x_n[:, t, c * P:(c + 1) * P], ident[:, :])
                    last.then_inc(x_transposed, 1)

            def project_queries(b, p, first):
                if p in (2, 5, 6, 7) or (first and p in (3, 4)):
                    pe.wait_ge(q_lo, PAIRS * b + p - 1)
                elif p in (3, 4):
                    pe.wait_ge(out_ready, QT * (b - 1) + p)
                if p == 0:
                    pe.wait_ge(xT_ready, DC * b + 3)
                cols = slice(p * P, (p + 1) * P)
                for c in range(DC):
                    if p == 0:
                        pe.wait_ge(x_split, DC * b + c + 1)
                    mm = three_passes(nc, ps_proj[Q_BANK[p]][:, :], (wq_s[:, 0, c, cols], wq_s[:, 1, c, cols]),
                                      (x_s[:, 0, c, :], x_s[:, 1, c, :]), c == 0, c == DC - 1)
                mm.then_inc(q_projected, 1)

            def scores(b, p, first):
                j = PAIRS * b + p
                pe.wait_ge(q_lo, j + 1)
                if p == 0:
                    pe.wait_ge(kb_split, 2 * b + 2)
                for h in range(2):
                    if not (first and p == 0):
                        pe.wait_ge(exp_ready, 2 * j + h - 1)
                    for t in range(2):
                        rows = slice((2 * h + t) * P, (2 * h + t + 1) * P)
                        mm = three_passes(nc, ps_s[h][:, t * W2:(t + 1) * W2],
                                          (q_s[:, p % 2, 0, rows], q_s[:, p % 2, 1, rows]),
                                          (k_s[:, 0, p, :], k_s[:, 1, p, :]), True, True)
                    mm.then_inc(scores_ready, 1)

            def transpose_probs(b, p, first):
                j = PAIRS * b + p
                pe.wait_ge(probs_ready, 2 * j + 2)
                for a in range(2):
                    if not (first and p == 0):
                        pe.wait_ge(pT_lo, 2 * j + a - 1)
                    for t in range(QT):
                        last = nc.tensor.transpose(ps_pT[a][0:KEYS, t * P:(t + 1) * P], prob[:, p % 2, t, a, :], ident[:, :])
                    last.then_inc(probs_transposed, 1)

            def weigh_values(b, p, first):
                j = PAIRS * b + p
                if not (first and p < 2):
                    pe.wait_ge(o_lo, j - 1)
                if p == 0:
                    pe.wait_ge(vb_split, b + 1)
                for a in range(2):
                    pe.wait_ge(pT_lo, 2 * j + a + 1)
                    cols = slice(a * DH, a * DH + P)
                    mm = three_passes(nc, ps_o[p % 2][:, :], (v_s[:, 0, p, cols], v_s[:, 1, p, cols]),
                                      (pT_s[:, p % 2, a, 0, :], pT_s[:, p % 2, a, 1, :]), a == 0, a == 1)
                mm.then_inc(o_ready, 1)

            def project_output(b, is_last):
                for t in range(QT):
                    if t == 0:
                        pe.wait_ge(o_lo, PAIRS * (b + 1))
                    if t < 2:
                        if not is_last:
                            pe.wait_ge(q_lo, PAIRS * (b + 1) + 2 + t)
                    else:
                        pe.wait_ge(out_ready, QT * b + t - 1)
                    rows = slice(t * P, (t + 1) * P)
                    for p in range(PAIRS):
                        mm = three_passes(nc, ps_proj[OUT_BANK[t]][:, :], (o_s[:, 0, p, rows], o_s[:, 1, p, rows]),
                                          (wo_s[:, 0, p, :], wo_s[:, 1, p, :]), p == 0, p == PAIRS - 1)
                    mm.then_inc(out_projected, 1)

            transpose_x(0, True)

            def batch(b, first, last):
                project_queries(b, 0, first)
                if not first:
                    transpose_probs(b - 1, 6, False)
                project_queries(b, 1, first)
                if not first:
                    transpose_probs(b - 1, 7, False)
                    weigh_values(b - 1, 6, False)
                scores(b, 0, first)
                project_queries(b, 2, first)
                if not first:
                    weigh_values(b - 1, 7, False)
                scores(b, 1, first)
                transpose_probs(b, 0, first)
                if not first:
                    project_output(b - 1, False)
                for p in range(3, PAIRS):
                    project_queries(b, p, first)
                    if p == 7 and not last:
                        transpose_x(b + 1, False)
                    scores(b, p - 1, first)
                    transpose_probs(b, p - 2, first)
                    weigh_values(b, p - 3, first)
                scores(b, 7, first)
                weigh_values(b, 5, first)

            batch(0, True, False)
            with pe.Fori(1, B - 1) as b:
                batch(b, False, False)
            batch(B - 1, False, True)
            transpose_probs(B - 1, 6, False)
            transpose_probs(B - 1, 7, False)
            weigh_values(B - 1, 6, False)
            weigh_values(B - 1, 7, False)
            project_output(B - 1, True)


def kernel(**inputs):
    import numpy as np
    import concourse.bacc as bacc
    from concourse.bass_utils import run_bass_kernel_spmd

    def columns(a):
        return np.ascontiguousarray(np.asarray(a).reshape(-1, P).T)

    layer = "L0_xattn_"
    arrays = {
        "x": inputs["x"], "ctx": inputs["ctx_1024"],
        "wq": inputs[layer + "Wq"], "bq": columns(inputs[layer + "bq"]),
        "wk": inputs[layer + "Wk"], "bk": columns(inputs[layer + "bk"]),
        "wv": inputs[layer + "Wv"], "bv": inputs[layer + "bv"],
        "wo": inputs[layer + "Wo"], "bo": inputs[layer + "bo"],
        "gamma": columns(inputs[layer + "ln_gamma"]), "beta": columns(inputs[layer + "ln_beta"]),
    }
    arrays = {f"in_{n}": np.ascontiguousarray(a) for n, a in arrays.items()}
    nc = bacc.Bacc("TRN2", target_bir_lowering=False, num_devices=1)
    args = [nc.dram_tensor(n, a.shape, mybir.dt.from_np(a.dtype), kind="ExternalInput").ap() for n, a in arrays.items()]
    out = nc.dram_tensor("out", inputs["x"].shape, F32, kind="ExternalOutput").ap()
    build_kernel(nc, *args, out)
    result = run_bass_kernel_spmd(nc, [arrays], core_ids=[0])
    return result.results[0]["out"]
```

```python
from contextlib import ExitStack

import concourse.bass as bass
from concourse import mybir

F32 = mybir.dt.float32
F32R = mybir.dt.float32r
ALU = mybir.AluOpType
ACT = mybir.ActivationFunctionType
AX_X = mybir.AxisListType.X

P = 128
EPS = 1e-5


def three_passes(nc, out, stationary, moving, first, last):
    (s_hi, s_lo), (m_hi, m_lo) = stationary, moving
    nc.tensor.matmul(out, s_hi, m_hi, start=first, stop=False)
    nc.tensor.matmul(out, s_hi, m_lo, start=False, stop=False)
    return nc.tensor.matmul(out, s_lo, m_hi, start=False, stop=last)


def offset(eng, value):
    return value if type(value) is int else eng.snap(value)


def build_kernel(nc, x, ctx_in, wq, bq, wk, bk, wv, bv, wo, bo, gamma, beta, out):
    B, S, D = x.shape
    KEYS = ctx_in.shape[1]
    H = wq.shape[1]
    DH = 64
    PAIRS = H // P
    DC = D // P
    QT = S // P
    ROWS = B * KEYS
    GROUP = 512
    GROUPS = -(-ROWS // GROUP)
    STEP = (ROWS - GROUP) // (GROUPS - 1)
    assert STEP * (GROUPS - 1) + GROUP == ROWS and STEP <= GROUP
    RT = GROUP // P
    HALF = H // 2
    W2 = 2 * KEYS
    K_SCALE = float(DH) ** -0.5
    assert K_SCALE == 0.125 and D == 512 and S == 512 and H == 1024

    k_dram = nc.dram_tensor("k_scratch", (PAIRS, P, ROWS), F32, kind="Internal").ap()
    v_dram = nc.dram_tensor("v_scratch", (ROWS, H), F32, kind="Internal").ap()
    ctx_rows = ctx_in.rearrange("b s d -> (b s) d")

    with ExitStack() as whole:
        def sem(name):
            return whole.enter_context(nc.semaphore(name))

        def sb(stack, name, shape, dt=F32):
            return stack.enter_context(nc.sbuf_tensor(name, shape, dt))

        banks = [whole.enter_context(nc.psum_tensor(f"bank{i}", [P, 512], F32)) for i in range(8)]

        wq_s = sb(whole, "wq_s", [P, 2, DC, H], F32R)
        wo_s = sb(whole, "wo_s", [P, 2, PAIRS, D], F32R)
        ident = sb(whole, "ident", [P, P])
        gam = sb(whole, "gam", [P, DC])
        bet = sb(whole, "bet", [P, DC])
        bq_c = sb(whole, "bq_c", [P, PAIRS])
        minus_half = sb(whole, "minus_half", [P, 4])
        eps_c = sb(whole, "eps_c", [P, 4])
        x_in = sb(whole, "x_in", [P, QT, D])
        x_n = sb(whole, "x_n", [P, QT, D])
        x_stats = sb(whole, "x_stats", [P, QT, 6])
        x_counts = sb(whole, "x_counts", [P, 1])
        x_mv = sb(whole, "x_mv", [P, QT, 2])
        x_var = sb(whole, "x_var", [P, QT])
        x_rstd = sb(whole, "x_rstd", [P, QT])

        x_loaded = sem("x_loaded")
        x_stats_done = sem("x_stats_done")
        x_counted = sem("x_counted")
        x_aggregated = sem("x_aggregated")
        x_var_eps = sem("x_var_eps")
        x_rstd_done = sem("x_rstd_done")
        x_normed = sem("x_normed")
        x_transposed = sem("x_transposed")
        xT_ready = sem("xT_ready")

        project_context(nc, sem, sb, banks, locals())
        attend(nc, sem, sb, banks, locals())


def x_statistics(nc, dve, g, b):
    for t in range(g["QT"]):
        dve.wait_ge(g["x_loaded"], 16 * (b + 1))
        nc.vector.bn_stats(g["x_stats"][:, t, :], g["x_in"][:, t, :]).then_inc(g["x_stats_done"], 1)


def x_aggregate(nc, dve, g, b):
    QT = g["QT"]
    dve.wait_ge(g["x_stats_done"], QT * (b + 1))
    nc.vector.tensor_copy(g["x_counts"][:, :], g["x_stats"][:, QT - 1, 0:1]).then_inc(g["x_counted"], 1)
    for t in range(QT):
        nc.vector.bn_aggr(g["x_mv"][:, t, :], g["x_stats"][:, t, :]).then_inc(g["x_aggregated"], 1)


def x_inverse_deviation(nc, pool, g, b):
    QT = g["QT"]
    pool.wait_ge(g["x_aggregated"], QT * (b + 1))
    pool.tensor_tensor(g["x_var"][:, :], g["x_mv"][:, :, 1], g["eps_c"][:, 0:QT], ALU.add).then_inc(g["x_var_eps"], 1)
    pool.wait_ge(g["x_var_eps"], b + 1)
    pool.tensor_tensor(g["x_rstd"][:, :], g["x_var"][:, :], g["minus_half"][:, 0:QT], ALU.pow).then_inc(g["x_rstd_done"], 1)


def x_normalise(nc, dve, g, b):
    for t in range(g["QT"]):
        dve.wait_ge(g["x_rstd_done"], b + 1)
        nc.vector.tensor_scalar(g["x_n"][:, t, :], g["x_in"][:, t, :], g["x_mv"][:, t, 0:1], g["x_rstd"][:, t:t + 1],
                                ALU.subtract, ALU.mult).then_inc(g["x_normed"], 1)


def project_context(nc, sem, sb, banks, g):
    B, D, H, PAIRS, DC, ROWS = g["B"], g["D"], g["H"], g["PAIRS"], g["DC"], g["ROWS"]
    GROUP, GROUPS, STEP, RT, K_SCALE = g["GROUP"], g["GROUPS"], g["STEP"], g["RT"], g["K_SCALE"]
    HALF = g["HALF"]
    wq_s, wo_s, ident, gam, bet, bq_c, minus_half, eps_c = (
        g["wq_s"], g["wo_s"], g["ident"], g["gam"], g["bet"], g["bq_c"], g["minus_half"], g["eps_c"])
    wq, wk, wv, wo, bq, bk, bv = g["wq"], g["wk"], g["wv"], g["wo"], g["bq"], g["bk"], g["bv"]
    k_dram, v_dram, ctx_rows = g["k_dram"], g["v_dram"], g["ctx_rows"]

    with ExitStack() as st:
        wk_s = sb(st, "wk_s", [P, 2, DC, H], F32R)
        wv_s = sb(st, "wv_s", [P, 2, DC, H], F32R)
        w_raw = sb(st, "w_raw", [P, 2, H])
        c_n = sb(st, "c_n", [P, RT, D])
        c_T = sb(st, "c_T", [P, 2, DC, P])
        c_s = sb(st, "c_s", [P, 2, DC, GROUP], F32R)
        k_st = sb(st, "k_st", [P, 2, GROUP])
        v_st = sb(st, "v_st", [P, 2, H])
        bv_b = sb(st, "bv_b", [P, H])
        bk_c = sb(st, "bk_c", [P, PAIRS])
        bk_8 = sb(st, "bk_8", [P, PAIRS])
        stats = sb(st, "c_stats", [P, RT, 6])
        mv = sb(st, "c_mv", [P, RT, 2])
        counts = sb(st, "c_counts", [P, 1])
        var_eps = sb(st, "c_var_eps", [P, RT])
        rstd = sb(st, "c_rstd", [P, RT])
        ps_k = [banks[0], banks[1]]
        ps_v = [[banks[2], banks[3]], [banks[4], banks[5]]]
        ps_t = [banks[6], banks[7]]

        consts_loaded = sem("consts_loaded")
        bv_loaded = sem("bv_loaded")
        ctx_loaded = [sem(f"ctx_loaded{t}") for t in range(RT)]
        w_loaded = [sem("w_loaded0"), sem("w_loaded1")]
        consts_made = sem("consts_made")
        w_rounded = sem("w_rounded")
        w_split = sem("w_split")
        bk_scaled = sem("bk_scaled")
        c_stats_done = sem("c_stats_done")
        c_aggregated = sem("c_aggregated")
        c_var_eps = sem("c_var_eps")
        c_counted = sem("c_counted")
        c_rstd_done = sem("c_rstd_done")
        c_normed = sem("c_normed")
        c_transposed = sem("c_transposed")
        cT_ready = sem("cT_ready")
        c_rounded = sem("c_rounded")
        c_split = sem("c_split")
        k_projected = sem("k_projected")
        k_ready = sem("k_ready")
        k_stored = [sem("k_stored0"), sem("k_stored1")]
        v_projected = sem("v_projected")
        v_ready = sem("v_ready")
        v_stored = [sem("v_stored0"), sem("v_stored1")]

        chunks = [(w.rearrange("(c p) n -> c p n", p=P)[c], [ws[:, i, c, :] for i in range(2)])
                  for w, ws in ((wv, wv_s), (wk, wk_s), (wq, wq_s)) for c in range(DC)]
        chunks += [(wo.rearrange("(c a p) n -> c p a n", p=P, a=2)[c],
                    [wo_s[:, i, 2 * c:2 * c + 2, :] for i in range(2)]) for c in range(PAIRS // 2)]
        EARLY = 2 * DC

        block = st.enter_context(nc.Block())

        @block.sync
        def _(sp):
            def load_context(row, t):
                sp.dma_start(c_n[:, t, :], ctx_rows[bass.ds(row, P), :]).then_inc(ctx_loaded[t], 16)

            def load_weight(n):
                if n >= 2:
                    sp.wait_ge(w_split, n - 1)
                dst = w_raw[:, n % 2, :]
                if n >= 3 * DC:
                    dst = dst.rearrange("p (a n) -> p a n", a=2)
                sp.dma_start(dst, chunks[n][0]).then_inc(w_loaded[n % 2], 16)

            load_context(0, 0)
            for dst, src in ((gam, g["gamma"]), (bet, g["beta"]), (bq_c, bq), (bk_c, bk)):
                sp.dma_start(dst[:, :], src).then_inc(consts_loaded, 16)
            for t in range(1, RT):
                load_context(t * P, t)
            for n in range(EARLY):
                load_weight(n)
            sp.dma_start(bv_b[:, :], bv.rearrange("(a n) -> a n", a=1).to_broadcast([P, H])).then_inc(bv_loaded, 16)

            def group(r, first, last):
                if not last:
                    next_rows = [offset(sp, r * STEP + STEP + t * P) for t in range(RT)]
                    for t in range(RT):
                        sp.wait_ge(c_transposed, RT * r + t + 1)
                        load_context(next_rows[t], t)
                if first:
                    for n in range(EARLY, len(chunks)):
                        load_weight(n)

            group(0, True, False)
            with sp.Fori(1, GROUPS - 1) as r:
                group(r, False, False)
            sp.dma_start(g["x_in"][:, :, :], g["x"].rearrange("b s d -> (b s) d")[0:g["S"], :].rearrange("(t p) d -> p t d", p=P)).then_inc(g["x_loaded"], 16)
            for s in range(2):
                sp.wait_ge(k_stored[s], 16 * (PAIRS // 2) * GROUPS)
                sp.wait_ge(v_stored[s], 16 * (RT // 2) * GROUPS)

        @block.gpsimd
        def _(pool):
            pool.memset(ident[:, :], 0.0).then_inc(consts_made, 1)
            pool.memset(minus_half[:, :], -0.5).then_inc(consts_made, 1)
            pool.memset(eps_c[:, :], EPS).then_inc(consts_made, 1)
            pool.wait_ge(consts_made, 3)
            pool.affine_select(out=ident[:, :], in_=ident[:, :], compare_op=ALU.not_equal, fill=1.0, base=0,
                               pattern=[[-1, P]], channel_multiplier=1).then_inc(consts_made, 1)

            def rstd_of(r):
                pool.wait_ge(c_aggregated, RT * (r + 1))
                pool.tensor_tensor(var_eps[:, :], mv[:, :, 1], eps_c[:, 0:RT], ALU.add).then_inc(c_var_eps, 1)
                pool.wait_ge(c_var_eps, r + 1)
                pool.tensor_tensor(rstd[:, :], var_eps[:, :], minus_half[:, 0:RT], ALU.pow).then_inc(c_rstd_done, 1)

            rstd_of(0)
            with pool.Fori(1, GROUPS) as r:
                rstd_of(r)
            x_inverse_deviation(nc, pool, g, 0)

        @block.vector
        def _(dve):
            def statistics(r):
                for t in range(RT):
                    dve.wait_ge(ctx_loaded[t], 16 * (r + 1))
                    nc.vector.bn_stats(stats[:, t, :], c_n[:, t, :]).then_inc(c_stats_done, 1)
                dve.wait_ge(c_stats_done, RT * (r + 1))
                nc.vector.tensor_copy(counts[:, :], stats[:, RT - 1, 0:1]).then_inc(c_counted, 1)
                for t in range(RT):
                    nc.vector.bn_aggr(mv[:, t, :], stats[:, t, :]).then_inc(c_aggregated, 1)

            def normalise(r):
                for t in range(RT):
                    dve.wait_ge(c_rstd_done, r + 1)
                    nc.vector.tensor_scalar(c_n[:, t, :], c_n[:, t, :], mv[:, t, 0:1], rstd[:, t:t + 1],
                                            ALU.subtract, ALU.mult).then_inc(c_normed, 1)

            def split_weight(n):
                raw = w_raw[:, n % 2, :]
                if n >= 3 * DC:
                    raw = raw.rearrange("p (a n) -> p a n", a=2)
                hi, lo = chunks[n][1]
                dve.wait_ge(w_loaded[n % 2], 16 * (n // 2 + 1))
                nc.vector.tensor_copy(hi, raw).then_inc(w_rounded, 1)
                dve.wait_ge(w_rounded, n + 1)
                nc.vector.tensor_tensor(lo, raw, hi.bitcast(F32), ALU.subtract).then_inc(w_split, 1)

            def split_context(r, t):
                cols = slice(t * P, (t + 1) * P)
                dve.wait_ge(cT_ready, (RT * r + t + 1) * DC)
                nc.vector.tensor_copy(c_s[:, 0, :, cols], c_T[:, t % 2]).then_inc(c_rounded, 1)
                dve.wait_ge(c_rounded, RT * r + t + 1)
                nc.vector.tensor_tensor(c_s[:, 1, :, cols], c_T[:, t % 2], c_s[:, 0, :, cols].bitcast(F32),
                                        ALU.subtract).then_inc(c_split, 1)

            dve.wait_ge(consts_loaded, 64)
            nc.vector.tensor_scalar(bk_8[:, :], bk_c[:, :], K_SCALE, None, ALU.mult).then_inc(bk_scaled, 1)
            statistics(0)
            normalise(0)
            split_weight(0)
            for t in range(RT):
                split_context(0, t)
                split_weight(1 + t)
            for n in range(1 + RT, EARLY):
                split_weight(n)
            dve.wait_ge(bv_loaded, 16)

            def add_bias(r, t, first):
                for n in range(2):
                    dve.wait_ge(v_projected, 2 * RT * r + 2 * t + n + 1)
                    if t >= 2:
                        dve.wait_ge(v_stored[t % 2], 16 * ((RT // 2) * r + 1))
                    elif not first:
                        dve.wait_ge(v_stored[t % 2], 16 * (RT // 2) * r)
                    nc.vector.tensor_tensor(v_st[:, t % 2, n * HALF:(n + 1) * HALF], ps_v[t % 2][n][:, :],
                                            bv_b[:, n * HALF:(n + 1) * HALF], ALU.add).then_inc(v_ready, 1)

            def group(r, first, last):
                add_bias(r, 0, first)
                if not last:
                    statistics(r + 1)
                    normalise(r + 1)
                else:
                    x_statistics(nc, dve, g, 0)
                    x_aggregate(nc, dve, g, 0)
                    x_normalise(nc, dve, g, 0)
                if first:
                    for m in range(PAIRS):
                        split_weight(EARLY + m)
                for t in range(RT):
                    if not last:
                        if t == 0:
                            dve.wait_ge(k_projected, PAIRS * (r + 1))
                        split_context(r + 1, t)
                    else:
                        dve.wait_ge(g["x_transposed"], t + 1)
                        nc.vector.tensor_scalar(g["x_in"][:, t, :], ps_t[t % 2][:, :], gam[:, t:t + 1], bet[:, t:t + 1],
                                                ALU.mult, ALU.add).then_inc(g["xT_ready"], 1)
                    if t < RT - 1:
                        add_bias(r, t + 1, first)

            group(0, True, False)
            with dve.Fori(1, GROUPS - 1) as r:
                group(r, False, False)
            group(GROUPS - 1, False, True)

        @block.scalar
        def _(act):
            def evacuate_transposed(r, t):
                act.wait_ge(c_transposed, RT * r + t + 1)
                for c in range(DC):
                    if c == 0:
                        if t >= 2:
                            act.wait_ge(c_split, RT * r + t - 1)
                        elif type(r) is not int or r > 0:
                            act.wait_ge(c_split, RT * r + t - 1)
                    nc.scalar.activation(c_T[:, t % 2, c, :], ps_t[t % 2][:, c * P:(c + 1) * P], ACT.Identity,
                                         bias=bet[:, c:c + 1], scale=gam[:, c:c + 1]).then_inc(cT_ready, 1)

            def store_values(r, rows, t):
                act.wait_ge(v_ready, 2 * RT * r + 2 * t + 2)
                act.dma_start(v_dram[bass.ds(rows[t], P), :], v_st[:, t % 2, :]).then_inc(v_stored[t % 2], 16)

            act.wait_ge(consts_loaded, 64)
            act.wait_ge(bk_scaled, 1)
            for t in range(RT):
                evacuate_transposed(0, t)

            def group(r, first, last):
                rows = [offset(act, r * STEP + t * P) for t in range(RT)]
                if not first:
                    act.wait_ge(v_stored[1], 16 * (RT // 2) * r)
                store_values(r, rows, 0)
                for m in range(PAIRS):
                    act.wait_ge(k_projected, PAIRS * r + m + 1)
                    if m >= 2:
                        act.wait_ge(k_stored[m % 2], 16 * ((PAIRS // 2) * r + m // 2))
                    elif not first:
                        act.wait_ge(k_stored[m % 2], 16 * (PAIRS // 2) * r)
                    nc.scalar.activation(k_st[:, m % 2, :], ps_k[m % 2][:, :], ACT.Identity,
                                         bias=bk_8[:, m:m + 1], scale=K_SCALE).then_inc(k_ready, 1)
                    act.wait_ge(k_ready, PAIRS * r + m + 1)
                    act.dma_start(k_dram[m, :, bass.ds(rows[0], GROUP)], k_st[:, m % 2, :]).then_inc(k_stored[m % 2], 16)
                for t in range(RT):
                    if not last:
                        evacuate_transposed(r + 1, t)
                    if t < RT - 1:
                        store_values(r, rows, t + 1)

            group(0, True, False)
            with act.Fori(1, GROUPS - 1) as r:
                group(r, False, False)
            group(GROUPS - 1, False, True)

        @block.tensor
        def _(pe):
            def transpose_tile(r, t, start):
                pe.wait_ge(c_normed, RT * r + t + 1)
                if not (start and t < 2):
                    pe.wait_ge(cT_ready, DC * (RT * r + t - 1))
                for c in range(DC):
                    last = nc.tensor.transpose(ps_t[t % 2][:, c * P:(c + 1) * P], c_n[:, t, c * P:(c + 1) * P],
                                               ident[:, :])
                last.then_inc(c_transposed, 1)

            def project_keys(r, first):
                pe.wait_ge(c_split, RT * (r + 1))
                for m in range(PAIRS):
                    if m >= 2 or not first:
                        pe.wait_ge(k_ready, PAIRS * r + m - 1)
                    cols = slice(m * P, (m + 1) * P)
                    for c in range(DC):
                        if first and m == 0:
                            pe.wait_ge(w_split, DC + c + 1)
                        mm = three_passes(nc, ps_k[m % 2][:, :], (wk_s[:, 0, c, cols], wk_s[:, 1, c, cols]),
                                          (c_s[:, 0, c, :], c_s[:, 1, c, :]), c == 0, c == DC - 1)
                    mm.then_inc(k_projected, 1)

            def project_values(r, t, first):
                rows = slice(t * P, (t + 1) * P)
                for n in range(2):
                    cols = slice(n * HALF, (n + 1) * HALF)
                    if t >= 2 or not first:
                        pe.wait_ge(v_ready, 2 * RT * r + 2 * t + n - 3)
                    if t == 0:
                        pe.wait_ge(c_split, RT * r + 1)
                    for c in range(DC):
                        if first and t == 0 and n == 0:
                            pe.wait_ge(w_split, c + 1)
                        mm = three_passes(nc, ps_v[t % 2][n][:, :], (c_s[:, 0, c, rows], c_s[:, 1, c, rows]),
                                          (wv_s[:, 0, c, cols], wv_s[:, 1, c, cols]), c == 0, c == DC - 1)
                    mm.then_inc(v_projected, 1)

            def transpose_x(c):
                pe.wait_ge(g["x_normed"], g["QT"])
                if c >= 2:
                    pe.wait_ge(g["xT_ready"], c - 1)
                for q in range(g["QT"]):
                    mm = nc.tensor.transpose(ps_t[c % 2][:, q * P:(q + 1) * P],
                                             g["x_n"][:, q, c * P:(c + 1) * P], ident[:, :])
                mm.then_inc(g["x_transposed"], 1)

            pe.wait_ge(consts_made, 4)
            for t in range(RT):
                transpose_tile(0, t, True)

            def group(r, first, last):
                project_values(r, 0, first)
                project_keys(r, first)
                for t in range(RT):
                    if last:
                        transpose_x(t)
                    else:
                        transpose_tile(r + 1, t, False)
                    if t < RT - 1:
                        project_values(r, t + 1, first)

            group(0, True, False)
            with pe.Fori(1, GROUPS - 1) as r:
                group(r, False, False)
            group(GROUPS - 1, False, True)


def attend(nc, sem, sb, banks, g):
    B, S, D, KEYS, H = g["B"], g["S"], g["D"], g["KEYS"], g["H"]
    DH, PAIRS, DC, QT, W2 = g["DH"], g["PAIRS"], g["DC"], g["QT"], g["W2"]
    wq_s, wo_s, ident, gam, bet, bq_c, minus_half, eps_c = (
        g["wq_s"], g["wo_s"], g["ident"], g["gam"], g["bet"], g["bq_c"], g["minus_half"], g["eps_c"])
    x, bo, out, k_dram, v_dram = g["x"], g["bo"], g["out"], g["k_dram"], g["v_dram"]
    x_in, x_n = g["x_in"], g["x_n"]
    x_loaded, x_normed, x_transposed, xT_ready = g["x_loaded"], g["x_normed"], g["x_transposed"], g["xT_ready"]

    x_rows = x.rearrange("b s d -> (b s) d")
    out_rows = out.rearrange("b s d -> (b s) d")
    KEYS_EARLY = 2
    PV = 3 * DH

    with ExitStack() as st:
        x_bo = sb(st, "x_bo", [P, QT, D])
        x_s = sb(st, "x_s", [P, 2, DC, S], F32R)
        q_s = sb(st, "q_s", [P, 2, 2, S], F32R)
        k_in = sb(st, "k_in", [P, PAIRS, KEYS])
        k_s = sb(st, "k_s", [P, 2, PAIRS, W2], F32R)
        v_in = sb(st, "v_in", [KEYS, PAIRS, 2, DH])
        v_s = sb(st, "v_s", [KEYS, 2, PAIRS, PV], F32R)
        prob = sb(st, "prob", [P, 2, QT, 2, KEYS])
        pT_s = sb(st, "pT_s", [KEYS, 2, 2, 2, S], F32R)
        o_s = sb(st, "o_s", [P, 2, PAIRS, S], F32R)
        o_out = sb(st, "o_out", [P, 2, D])
        bo_b = sb(st, "bo_b", [P, D])
        neg_max = sb(st, "neg_max", [P, 2, QT, 2])
        sums = sb(st, "sums", [P, 2, QT, 2])
        recip = sb(st, "recip", [P, 2, QT, 2])
        v_halves = [v_s[:, i].rearrange("k m (a d) -> k m a d", a=3)[:, :, 0:3:2, :] for i in range(2)]
        ps_proj = [banks[0], banks[1]]
        ps_s = [banks[2], banks[3]]
        ps_pT = [banks[4], banks[5]]
        ps_o = [banks[6], banks[7]]

        bo_loaded = sem("bo_loaded")
        x_reloaded = sem("x_reloaded")
        k_loaded = sem("k_loaded")
        v_loaded = sem("v_loaded")
        zeroed = sem("zeroed")
        residual_ready = sem("residual_ready")
        x_rounded = sem("x_rounded")
        x_split_v = sem("x_split_v")
        x_split_g = sem("x_split_g")
        kb_rounded = sem("kb_rounded")
        kb_split = sem("kb_split")
        vb_rounded = sem("vb_rounded")
        vb_split = sem("vb_split")
        q_projected = sem("q_projected")
        q_hi = sem("q_hi")
        q_lo = sem("q_lo")
        scores_ready = sem("scores_ready")
        max_ready = sem("max_ready")
        exp_ready = sem("exp_ready")
        recip_ready = sem("recip_ready")
        probs_ready = sem("probs_ready")
        probs_transposed = sem("probs_transposed")
        pT_hi = sem("pT_hi")
        pT_lo = sem("pT_lo")
        o_ready = sem("o_ready")
        o_hi = sem("o_hi")
        o_lo = sem("o_lo")
        out_projected = sem("out_projected")
        out_ready = sem("out_ready")
        out_stored = [sem("out_stored0"), sem("out_stored1")]

        Q_BANK = [0, 1, 0, 1, 1, 1, 1, 1]
        OUT_BANK = [1, 0, 1, 0]

        block = st.enter_context(nc.Block())


        @block.sync
        def _(sp):
            def load_x(row, dst, loaded):
                sp.dma_start(dst[:, :, :], x_rows[bass.ds(row, S), :].rearrange("(t p) d -> p t d", p=P)).then_inc(loaded, 16)

            def load_k(key):
                sp.dma_start(k_in[:, :, :], k_dram[:, :, bass.ds(key, KEYS)].rearrange("m p c -> p m c")).then_inc(k_loaded, 16)

            def load_v(key):
                sp.dma_start(v_in[:, :, :, :], v_dram[bass.ds(key, KEYS), :].rearrange("k (m a d) -> k m a d", m=PAIRS, a=2)).then_inc(v_loaded, 16)

            def store_out(b, rows):
                for t in range(QT):
                    sp.wait_ge(out_ready, QT * b + t + 1)
                    sp.dma_start(out_rows[bass.ds(rows[t], P), :], o_out[:, t % 2, :]).then_inc(out_stored[t % 2], 16)

            sp.dma_start(bo_b[:, :], bo.rearrange("(a n) -> a n", a=1).to_broadcast([P, D])).then_inc(bo_loaded, 16)
            load_k(0)
            load_v(0)
            load_x(0, x_bo, x_reloaded)

            def batch(b, first, last):
                if not last:
                    next_row, next_key = offset(sp, b * S + S), offset(sp, b * KEYS + KEYS)
                if not first:
                    row = offset(sp, b * S)
                    out_row = [offset(sp, b * S + (t * P - S)) for t in range(QT)]
                if not last:
                    sp.wait_ge(x_split_v, DC // 2 * (b + 1))
                    sp.wait_ge(x_split_g, DC // 2 * (b + 1))
                    load_x(next_row, x_in, x_loaded)
                    sp.wait_ge(kb_split, 4 * b + 4)
                    load_k(next_key)
                    sp.wait_ge(vb_split, b + 1)
                    load_v(next_key)
                if not first:
                    store_out(b - 1, out_row)
                    load_x(row, x_bo, x_reloaded)

            batch(0, True, False)
            with sp.Fori(1, B - 1) as b:
                batch(b, False, False)
            batch(B - 1, False, True)
            store_out(B - 1, [(B - 1) * S + t * P for t in range(QT)])
            for s in range(2):
                sp.wait_ge(out_stored[s], 16 * (QT // 2) * B)

        @block.gpsimd
        def _(pool):
            def x_low(b):
                for c in range(DC // 2):
                    pool.wait_ge(x_rounded, DC * b + c + 1)
                    pool.tensor_tensor(x_s[:, 1, c, :], x_in[:, c, :], x_s[:, 0, c, :].bitcast(F32),
                                       ALU.subtract).then_inc(x_split_g, 1)

            def residual(b, tiles):
                for t in tiles:
                    pool.wait_ge(x_reloaded, 16 * (b + 1))
                    pool.tensor_tensor(x_bo[:, t, :], x_bo[:, t, :], bo_b[:, :], ALU.add).then_inc(residual_ready, 1)

            def values_low(b):
                pool.wait_ge(vb_rounded, b + 1)
                pool.tensor_tensor(v_halves[1], v_in[:, :, :, :], v_halves[0].bitcast(F32), ALU.subtract).then_inc(vb_split, 1)

            def divide(b, p):
                for h in range(2):
                    pr = prob[:, p % 2, 2 * h:2 * h + 2].rearrange("p t a k -> p (t a) k")
                    rc = recip[:, p % 2, 2 * h:2 * h + 2].rearrange("p t a -> p (t a)")
                    pool.wait_ge(recip_ready, 2 * (PAIRS * b + p) + h + 1)
                    pool.tensor_tensor(pr, pr, rc[:, :, None].to_broadcast([P, 4, KEYS]), ALU.mult).then_inc(probs_ready, 1)

            x_low(0)
            pool.memset(k_s[:, :, :, :].bitcast(F32), 0.0).then_inc(zeroed, 1)
            pool.memset(v_s[:, :, :, :].bitcast(F32), 0.0).then_inc(zeroed, 1)
            pool.wait_ge(bo_loaded, 16)
            pool.wait_ge(zeroed, 2)

            def batch(b, first, last):
                if not first:
                    divide(b - 1, 7)
                for p in range(1, PAIRS):
                    if p == 7 and not last:
                        x_low(b + 1)
                    divide(b, p - 1)
                    if p == 2:
                        if not first:
                            residual(b - 1, [0, 1])
                        values_low(b)
                        if not last:
                            x_inverse_deviation(nc, pool, g, b + 1)
                        if not first:
                            residual(b - 1, [2, 3])

            batch(0, True, False)
            with pool.Fori(1, B - 1) as b:
                batch(b, False, False)
            batch(B - 1, False, True)
            divide(B - 1, 7)
            residual(B - 1, range(QT))

        @block.vector
        def _(dve):
            def statistics(b):
                x_statistics(nc, dve, g, b)

            def aggregate(b):
                x_aggregate(nc, dve, g, b)

            def normalise_x(b):
                x_normalise(nc, dve, g, b)

            def values_high(b, first):
                dve.wait_ge(v_loaded, 16 * (b + 1))
                if not first:
                    dve.wait_ge(o_ready, PAIRS * b)
                nc.vector.tensor_copy(v_halves[0], v_in[:, :, :, :]).then_inc(vb_rounded, 1)

            def shift_x(b, c):
                dve.wait_ge(x_transposed, DC * b + c + 1)
                nc.vector.tensor_scalar(x_in[:, c, :], ps_proj[0][:, :], gam[:, c:c + 1], bet[:, c:c + 1],
                                        ALU.mult, ALU.add).then_inc(xT_ready, 1)

            def round_x(b, chunks):
                dve.wait_ge(q_projected, PAIRS * b)
                for c in chunks:
                    dve.wait_ge(xT_ready, DC * b + c + 1)
                    nc.vector.tensor_copy(x_s[:, 0, c, :], x_in[:, c, :]).then_inc(x_rounded, 1)

            def x_low(b, chunks):
                for c in chunks:
                    dve.wait_ge(x_rounded, DC * b + c + 1)
                    nc.vector.tensor_tensor(x_s[:, 1, c, :], x_in[:, c, :], x_s[:, 0, c, :].bitcast(F32),
                                            ALU.subtract).then_inc(x_split_v, 1)

            def split_keys(b, part, used):
                pairs = slice(0, KEYS_EARLY) if part == 0 else slice(KEYS_EARLY, PAIRS)
                for a in range(2):
                    rows, cols = slice(a * DH, (a + 1) * DH), slice(a * KEYS, (a + 1) * KEYS)
                    dve.wait_ge(k_loaded, 16 * (b + 1))
                    if used is not None:
                        dve.wait_ge(scores_ready, used)
                    nc.vector.tensor_copy(k_s[rows, 0, pairs, cols], k_in[rows, pairs]).then_inc(kb_rounded, 1)
                for a in range(2):
                    rows, cols = slice(a * DH, (a + 1) * DH), slice(a * KEYS, (a + 1) * KEYS)
                    dve.wait_ge(kb_rounded, 4 * b + 2 * part + a + 1)
                    nc.vector.tensor_tensor(k_s[rows, 1, pairs, cols], k_in[rows, pairs],
                                            k_s[rows, 0, pairs, cols].bitcast(F32), ALU.subtract).then_inc(kb_split, 1)

            def query_low(b, p):
                j = PAIRS * b + p
                dve.wait_ge(q_hi, j + 1)
                nc.vector.scalar_tensor_tensor(out=q_s[:, p % 2, 1, :], in0=ps_proj[Q_BANK[p]][:, :],
                                               scalar=bq_c[:, p:p + 1], in1=q_s[:, p % 2, 0, :].bitcast(F32),
                                               op0=ALU.add, op1=ALU.subtract).then_inc(q_lo, 1)

            def maxima(b, p, halves):
                for h in halves:
                    dve.wait_ge(scores_ready, 2 * (PAIRS * b + p) + h + 1)
                    nc.vector.tensor_reduce(neg_max[:, p % 2, 2 * h:2 * h + 2, :].rearrange("p t a -> p (t a)"),
                                            ps_s[h][:, 0:2 * W2].rearrange("p (t k) -> p t k", k=KEYS),
                                            AX_X, ALU.max, negate=True).then_inc(max_ready, 1)

            def reciprocals(b, p):
                for h in range(2):
                    dve.wait_ge(exp_ready, 2 * (PAIRS * b + p) + h + 1)
                    nc.vector.reciprocal(recip[:, p % 2, 2 * h:2 * h + 2, :], sums[:, p % 2, 2 * h:2 * h + 2, :]).then_inc(recip_ready, 1)

            def probs_low(b, p):
                for a in range(2):
                    dve.wait_ge(pT_hi, 2 * (PAIRS * b + p) + a + 1)
                    nc.vector.tensor_tensor(pT_s[:, p % 2, a, 1, :], ps_pT[a][0:KEYS, :],
                                            pT_s[:, p % 2, a, 0, :].bitcast(F32), ALU.subtract).then_inc(pT_lo, 1)

            def output_low(b, p):
                dve.wait_ge(o_hi, PAIRS * b + p + 1)
                nc.vector.tensor_tensor(o_s[:, 1, p, :], ps_o[p % 2][:, :], o_s[:, 0, p, :].bitcast(F32),
                                        ALU.subtract).then_inc(o_lo, 1)

            def add_residual(b, tiles):
                for t in tiles:
                    dve.wait_ge(out_projected, QT * b + t + 1)
                    dve.wait_ge(residual_ready, QT * b + t + 1)
                    if t >= 2:
                        dve.wait_ge(out_stored[t % 2], 16 * ((QT // 2) * b + 1))
                    nc.vector.tensor_tensor(o_out[:, t % 2, :], ps_proj[OUT_BANK[t]][:, :], x_bo[:, t, :],
                                            ALU.add).then_inc(out_ready, 1)

            for c in range(DC):
                nc.vector.tensor_copy(x_s[:, 0, c, :], x_in[:, c, :]).then_inc(x_rounded, 1)
            x_low(0, range(DC // 2, DC))
            dve.wait_ge(zeroed, 2)
            split_keys(0, 0, None)

            def batch(b, first, last):
                for p in range(PAIRS):
                    one, two, three = (None if first and p < lag else (b - (p < lag), (p - lag) % PAIRS) for lag in (1, 2, 3))
                    if p == 6 and not first:
                        for s in range(2):
                            dve.wait_ge(out_stored[s], 16 * (QT // 2) * b)
                    if one:
                        maxima(*one, [0])
                    if p < 7:
                        query_low(b, p)
                    elif not last:
                        x_low(b + 1, [3])
                    if p == 2 and not first:
                        output_low(*three)
                    if one:
                        maxima(*one, [1])
                    if p == 7:
                        query_low(b, 7)
                    if 3 <= p < 3 + DC and not last:
                        shift_x(b + 1, p - 3)
                    if p == 3 and not last:
                        split_keys(b + 1, 0, 2 * (PAIRS * b + KEYS_EARLY))
                    if one:
                        reciprocals(*one)
                    if two:
                        probs_low(*two)
                    if p == 6 and not last:
                        round_x(b + 1, range(DC))
                        x_low(b + 1, [2])
                    if p != 2 and three:
                        output_low(*three)
                    if p == 2:
                        split_keys(b, 1, None if first else 2 * PAIRS * b)
                        values_high(b, first)
                        if not last:
                            statistics(b + 1)
                            aggregate(b + 1)
                        if not first:
                            add_residual(b - 1, [0])
                        if not last:
                            normalise_x(b + 1)
                        if not first:
                            add_residual(b - 1, range(1, QT))

            batch(0, True, False)
            with dve.Fori(1, B - 1) as b:
                batch(b, False, False)
            batch(B - 1, False, True)
            maxima(B - 1, 7, range(2))
            reciprocals(B - 1, 7)
            probs_low(B - 1, 6)
            output_low(B - 1, 5)
            probs_low(B - 1, 7)
            output_low(B - 1, 6)
            output_low(B - 1, 7)
            add_residual(B - 1, range(QT))

        @block.scalar
        def _(act):
            def query_high(b, p, first):
                j = PAIRS * b + p
                act.wait_ge(q_projected, j + 1)
                if not (first and p < 2):
                    act.wait_ge(scores_ready, 2 * j - 2)
                nc.scalar.activation(q_s[:, p % 2, 0, :], ps_proj[Q_BANK[p]][:, :], ACT.Identity,
                                     bias=bq_c[:, p:p + 1]).then_inc(q_hi, 1)

            def exponentials(b, p, first):
                j = PAIRS * b + p
                if not (first and p < 2):
                    act.wait_ge(probs_transposed, 2 * j - 2)
                for h in range(2):
                    act.wait_ge(max_ready, 2 * j + h + 1)
                    for n in range(4):
                        t, a = 2 * h + n // 2, n % 2
                        last = nc.scalar.activation(prob[:, p % 2, t, a, :], ps_s[h][:, n * KEYS:(n + 1) * KEYS], ACT.Exp,
                                                    bias=neg_max[:, p % 2, t, a:a + 1],
                                                    accum_out=sums[:, p % 2, t, a:a + 1])
                    last.then_inc(exp_ready, 1)

            def probs_high(b, p, first):
                j = PAIRS * b + p
                for a in range(2):
                    act.wait_ge(probs_transposed, 2 * j + a + 1)
                    if not (first and p < 2):
                        act.wait_ge(o_ready, j - 1)
                    nc.scalar.activation(pT_s[:, p % 2, a, 0, :], ps_pT[a][0:KEYS, :], ACT.Copy).then_inc(pT_hi, 1)

            def output_high(b, p, first):
                act.wait_ge(o_ready, PAIRS * b + p + 1)
                if p == 0 and not first:
                    act.wait_ge(out_projected, QT * b)
                nc.scalar.activation(o_s[:, 0, p, :], ps_o[p % 2][:, :], ACT.Copy).then_inc(o_hi, 1)

            def batch(b, first, last):
                for p in range(PAIRS):
                    one, two, three = (None if first and p < lag else (b - (p < lag), (p - lag) % PAIRS) for lag in (1, 2, 3))
                    if p < 7:
                        query_high(b, p, first)
                    if p == 2 and not first:
                        output_high(*three, first)
                    if one:
                        exponentials(*one, first)
                    if two:
                        probs_high(*two, first)
                    if p == 6:
                        query_high(b, 7, first)
                    if p != 2 and three:
                        output_high(*three, first)

            batch(0, True, False)
            with act.Fori(1, B - 1) as b:
                batch(b, False, False)
            batch(B - 1, False, True)
            exponentials(B - 1, 7, False)
            probs_high(B - 1, 6, False)
            output_high(B - 1, 5, False)
            probs_high(B - 1, 7, False)
            output_high(B - 1, 6, False)
            output_high(B - 1, 7, False)

        @block.tensor
        def _(pe):
            def transpose_x(b, c, first):
                if c == 0:
                    pe.wait_ge(x_normed, QT * (b + 1))
                    if first:
                        pe.wait_ge(q_lo, 3)
                    else:
                        pe.wait_ge(out_ready, QT * (b - 1))
                else:
                    pe.wait_ge(xT_ready, DC * b + c)
                for t in range(QT):
                    last = nc.tensor.transpose(ps_proj[0][:, t * P:(t + 1) * P],
                                               x_n[:, t, c * P:(c + 1) * P], ident[:, :])
                last.then_inc(x_transposed, 1)

            def project_queries(b, p, first):
                if p == 0:
                    pe.wait_ge(xT_ready, DC * (b + 1))
                elif p == 3 and not first:
                    pe.wait_ge(out_ready, QT * (b - 1) + 3)
                elif p == 1 and not first:
                    pe.wait_ge(q_lo, PAIRS * b)
                elif p == 2:
                    pe.wait_ge(q_lo, PAIRS * b + 1)
                elif p >= 4 or p == 3:
                    pe.wait_ge(q_lo, PAIRS * b + (2 if p == 3 else p))
                cols = slice(p * P, (p + 1) * P)
                for c in range(DC):
                    if p == 0:
                        pe.wait_ge((x_split_g, x_split_v)[c // 2], DC // 2 * b + c % 2 + 1)
                    mm = three_passes(nc, ps_proj[Q_BANK[p]][:, :], (wq_s[:, 0, c, cols], wq_s[:, 1, c, cols]),
                                      (x_s[:, 0, c, :], x_s[:, 1, c, :]), c == 0, c == DC - 1)
                mm.then_inc(q_projected, 1)

            def score(b, p, n, first):
                j = PAIRS * b + p
                t, way = n // 3, n % 3
                h = t // 2
                if n == 0:
                    pe.wait_ge(q_lo, j + 1)
                    if p == 0:
                        pe.wait_ge(kb_split, 4 * b + 2)
                    if p == KEYS_EARLY:
                        pe.wait_ge(kb_split, 4 * b + 4)
                if n % 6 == 0 and not (first and p == 0):
                    pe.wait_ge(exp_ready, 2 * j + h - 1)
                q_part, k_part = ((0, 0), (0, 1), (1, 0))[way]
                mm = nc.tensor.matmul(ps_s[h][:, (t % 2) * W2:(t % 2 + 1) * W2], q_s[:, p % 2, q_part, t * P:(t + 1) * P],
                                      k_s[:, k_part, p, :], start=way == 0, stop=way == 2)
                if n % 6 == 5:
                    mm.then_inc(scores_ready, 1)

            def transpose_prob(b, p, n, first):
                j = PAIRS * b + p
                a, t = n // QT, n % QT
                if n == 0:
                    pe.wait_ge(probs_ready, 2 * j + 2)
                if t == 0 and not (first and p == 0):
                    pe.wait_ge(pT_lo, 2 * j + a - 1)
                mm = nc.tensor.transpose(ps_pT[a][0:KEYS, t * P:(t + 1) * P], prob[:, p % 2, t, a, :], ident[:, :])
                if t == QT - 1:
                    mm.then_inc(probs_transposed, 1)

            def scores(b, p, first):
                for n in range(3 * QT):
                    score(b, p, n, first)

            def transpose_probs(b, p, first):
                for n in range(2 * QT):
                    transpose_prob(b, p, n, first)

            def scores_and_transposes(b, p, b2, p2, first):
                ahead = QT
                for n in range(3 * QT):
                    score(b, p, n, first)
                    if n >= ahead:
                        transpose_prob(b2, p2, n - ahead, first)

            def weigh_values(b, p, first):
                j = PAIRS * b + p
                if not (first and p < 2):
                    pe.wait_ge(o_lo, j - 1)
                if p == 0:
                    pe.wait_ge(vb_split, b + 1)
                for a in range(2):
                    pe.wait_ge(pT_lo, 2 * j + a + 1)
                    cols = slice(a * DH, a * DH + P)
                    mm = three_passes(nc, ps_o[p % 2][:, :], (v_s[:, 0, p, cols], v_s[:, 1, p, cols]),
                                      (pT_s[:, p % 2, a, 0, :], pT_s[:, p % 2, a, 1, :]), a == 0, a == 1)
                mm.then_inc(o_ready, 1)

            def project_output(b, is_last):
                for t in range(QT):
                    if t < 2:
                        if not is_last:
                            pe.wait_ge(q_lo, PAIRS * (b + 1) + 2 + t)
                    else:
                        pe.wait_ge(out_ready, QT * b + t - 1)
                    rows = slice(t * P, (t + 1) * P)
                    for p in range(PAIRS):
                        if t == 0 and p == 0:
                            pe.wait_ge(o_lo, PAIRS * (b + 1) - 1)
                        elif t == 0 and p == PAIRS - 1:
                            pe.wait_ge(o_lo, PAIRS * (b + 1))
                        mm = three_passes(nc, ps_proj[OUT_BANK[t]][:, :], (o_s[:, 0, p, rows], o_s[:, 1, p, rows]),
                                          (wo_s[:, 0, p, :], wo_s[:, 1, p, :]), p == 0, p == PAIRS - 1)
                    mm.then_inc(out_projected, 1)

            def batch(b, first, last):
                for p in range(PAIRS):
                    one, two, three = (None if first and p < lag else (b - (p < lag), (p - lag) % PAIRS) for lag in (1, 2, 3))
                    if p < 7:
                        project_queries(b, p, first)
                    if p == 2 and not first:
                        weigh_values(*three, first)
                    if two:
                        scores_and_transposes(*one, *two, first)
                    elif one:
                        scores(*one, first)
                    if 3 <= p < 3 + DC and not last:
                        transpose_x(b + 1, p - 3, first)
                    if p == 6:
                        project_queries(b, 7, first)
                    if p != 2 and three:
                        weigh_values(*three, first)
                    if p == 2 and not first:
                        project_output(b - 1, False)

            batch(0, True, False)
            with pe.Fori(1, B - 1) as b:
                batch(b, False, False)
            batch(B - 1, False, True)
            scores_and_transposes(B - 1, 7, B - 1, 6, False)
            weigh_values(B - 1, 5, False)
            transpose_probs(B - 1, 7, False)
            weigh_values(B - 1, 6, False)
            weigh_values(B - 1, 7, False)
            project_output(B - 1, True)


def kernel(**inputs):
    import numpy as np
    import concourse.bacc as bacc
    from concourse.bass_utils import run_bass_kernel_spmd

    def columns(a):
        return np.ascontiguousarray(np.asarray(a).reshape(-1, P).T)

    layer = "L0_xattn_"
    arrays = {
        "x": inputs["x"], "ctx": inputs["ctx_1024"],
        "wq": inputs[layer + "Wq"], "bq": columns(inputs[layer + "bq"]),
        "wk": inputs[layer + "Wk"], "bk": columns(inputs[layer + "bk"]),
        "wv": inputs[layer + "Wv"], "bv": inputs[layer + "bv"],
        "wo": inputs[layer + "Wo"], "bo": inputs[layer + "bo"],
        "gamma": columns(inputs[layer + "ln_gamma"]), "beta": columns(inputs[layer + "ln_beta"]),
    }
    arrays = {f"in_{n}": np.ascontiguousarray(a) for n, a in arrays.items()}
    nc = bacc.Bacc("TRN2", target_bir_lowering=False, num_devices=1)
    args = [nc.dram_tensor(n, a.shape, mybir.dt.from_np(a.dtype), kind="ExternalInput").ap() for n, a in arrays.items()]
    out = nc.dram_tensor("out", inputs["x"].shape, F32, kind="ExternalOutput").ap()
    build_kernel(nc, *args, out)
    result = run_bass_kernel_spmd(nc, [arrays], core_ids=[0])
    return result.results[0]["out"]
```

```python
from contextlib import ExitStack

import concourse.bass as bass
from concourse import mybir

F32 = mybir.dt.float32
F32R = mybir.dt.float32r
ALU = mybir.AluOpType
ACT = mybir.ActivationFunctionType
AX_X = mybir.AxisListType.X

P = 128
EPS = 1e-5


def three_passes(nc, out, stationary, moving, first, last):
    (s_hi, s_lo), (m_hi, m_lo) = stationary, moving
    nc.tensor.matmul(out, s_hi, m_hi, start=first, stop=False)
    nc.tensor.matmul(out, s_hi, m_lo, start=False, stop=False)
    return nc.tensor.matmul(out, s_lo, m_hi, start=False, stop=last)


def offset(eng, value):
    return value if type(value) is int else eng.snap(value)


def build_kernel(nc, x, ctx_in, wq, bq, wk, bk, wv, bv, wo, bo, gamma, beta, out):
    B, S, D = x.shape
    KEYS = ctx_in.shape[1]
    H = wq.shape[1]
    DH = 64
    PAIRS = H // P
    DC = D // P
    QT = S // P
    ROWS = B * KEYS
    GROUP = 512
    GROUPS = -(-ROWS // GROUP)
    STEP = (ROWS - GROUP) // (GROUPS - 1)
    assert STEP * (GROUPS - 1) + GROUP == ROWS and STEP <= GROUP
    RT = GROUP // P
    HALF = H // 2
    W2 = 2 * KEYS
    K_SCALE = float(DH) ** -0.5
    assert K_SCALE == 0.125 and D == 512 and S == GROUP == 512 and H == 1024

    k_dram = nc.dram_tensor("k_scratch", (PAIRS, P, ROWS), F32, kind="Internal").ap()
    v_dram = nc.dram_tensor("v_scratch", (ROWS, H), F32, kind="Internal").ap()
    ctx_rows = ctx_in.rearrange("b s d -> (b s) d")

    with ExitStack() as whole:
        def sem(name):
            return whole.enter_context(nc.semaphore(name))

        def sb(stack, name, shape, dt=F32):
            return stack.enter_context(nc.sbuf_tensor(name, shape, dt))

        banks = [whole.enter_context(nc.psum_tensor(f"bank{i}", [P, 512], F32)) for i in range(8)]

        wq_s = sb(whole, "wq_s", [P, 2, DC, H], F32R)
        wo_s = sb(whole, "wo_s", [P, 2, PAIRS, D], F32R)
        ident = sb(whole, "ident", [P, P])
        gam = sb(whole, "gam", [P, DC])
        bet = sb(whole, "bet", [P, DC])
        bq_c = sb(whole, "bq_c", [P, PAIRS])
        minus_half = sb(whole, "minus_half", [P, 4])
        eps_c = sb(whole, "eps_c", [P, 4])
        x_in = sb(whole, "x_in", [P, QT, D])
        x_n = sb(whole, "x_n", [P, QT, D])
        x_s = sb(whole, "x_s", [P, 2, DC, S], F32R)
        k_in = sb(whole, "k_in", [P, PAIRS, KEYS])
        x_stats = sb(whole, "x_stats", [P, QT, 6])
        x_counts = sb(whole, "x_counts", [P, 1])
        x_mv = sb(whole, "x_mv", [P, QT, 2])
        x_var = sb(whole, "x_var", [P, QT])
        x_rstd = sb(whole, "x_rstd", [P, QT])

        x_loaded = sem("x_loaded")
        x_stats_done = sem("x_stats_done")
        x_counted = sem("x_counted")
        x_aggregated = sem("x_aggregated")
        x_var_eps = sem("x_var_eps")
        x_rstd_done = sem("x_rstd_done")
        x_normed = sem("x_normed")
        x_transposed = sem("x_transposed")
        xT_ready = sem("xT_ready")
        k_loaded = sem("k_loaded")
        x_rounded = sem("x_rounded")
        x_split_v = sem("x_split_v")
        x_split_g = sem("x_split_g")
        q_projected = sem("q_projected")

        project_context(nc, sem, sb, banks, locals())
        attend(nc, sem, sb, banks, locals())


def load_keys(sp, g, key):
    sp.dma_start(g["k_in"][:, :, :], g["k_dram"][:, :, bass.ds(key, g["KEYS"])].rearrange("m p c -> p m c")).then_inc(g["k_loaded"], 16)


def x_statistics(nc, dve, g, b, tiles):
    for t in tiles:
        dve.wait_ge(g["x_loaded"], 16 * (b + 1))
        nc.vector.bn_stats(g["x_stats"][:, t, :], g["x_in"][:, t, :]).then_inc(g["x_stats_done"], 1)


def x_aggregate(nc, dve, g, b):
    QT = g["QT"]
    dve.wait_ge(g["x_stats_done"], QT * (b + 1))
    nc.vector.tensor_copy(g["x_counts"][:, :], g["x_stats"][:, QT - 1, 0:1]).then_inc(g["x_counted"], 1)
    for t in range(QT):
        nc.vector.bn_aggr(g["x_mv"][:, t, :], g["x_stats"][:, t, :]).then_inc(g["x_aggregated"], 1)


def x_inverse_deviation(pool, g, b):
    QT = g["QT"]
    pool.wait_ge(g["x_aggregated"], QT * (b + 1))
    pool.tensor_tensor(g["x_var"][:, :], g["x_mv"][:, :, 1], g["eps_c"][:, 0:QT], ALU.add).then_inc(g["x_var_eps"], 1)
    pool.wait_ge(g["x_var_eps"], b + 1)
    pool.tensor_tensor(g["x_rstd"][:, :], g["x_var"][:, :], g["minus_half"][:, 0:QT], ALU.pow).then_inc(g["x_rstd_done"], 1)


def x_normalise(nc, dve, g, b):
    for t in range(g["QT"]):
        dve.wait_ge(g["x_rstd_done"], b + 1)
        nc.vector.tensor_scalar(g["x_n"][:, t, :], g["x_in"][:, t, :], g["x_mv"][:, t, 0:1], g["x_rstd"][:, t:t + 1],
                                ALU.subtract, ALU.mult).then_inc(g["x_normed"], 1)


def x_round(nc, dve, g, b, chunks):
    for c in chunks:
        dve.wait_ge(g["xT_ready"], g["DC"] * b + c + 1)
        nc.vector.tensor_copy(g["x_s"][:, 0, c, :], g["x_in"][:, c, :]).then_inc(g["x_rounded"], 1)


def x_low(eng, g, b, chunks, done):
    for c in chunks:
        eng.wait_ge(g["x_rounded"], g["DC"] * b + c + 1)
        eng.tensor_tensor(g["x_s"][:, 1, c, :], g["x_in"][:, c, :], g["x_s"][:, 0, c, :].bitcast(F32),
                          ALU.subtract).then_inc(done, 1)


def project_first_queries(nc, pe, g, bank, b):
    DC, wq_s, x_s = g["DC"], g["wq_s"], g["x_s"]
    for c in range(DC):
        pe.wait_ge(g["x_split_g"] if c < DC // 2 else g["x_split_v"], DC // 2 * b + c % 2 + 1)
        mm = three_passes(nc, bank[:, :], (wq_s[:, 0, c, 0:P], wq_s[:, 1, c, 0:P]),
                          (x_s[:, 0, c, :], x_s[:, 1, c, :]), c == 0, c == DC - 1)
    mm.then_inc(g["q_projected"], 1)


def project_context(nc, sem, sb, banks, g):
    D, H, PAIRS, DC = g["D"], g["H"], g["PAIRS"], g["DC"]
    GROUP, GROUPS, STEP, RT, K_SCALE = g["GROUP"], g["GROUPS"], g["STEP"], g["RT"], g["K_SCALE"]
    HALF = g["HALF"]
    wq_s, wo_s, ident, gam, bet, bq_c, minus_half, eps_c = (
        g["wq_s"], g["wo_s"], g["ident"], g["gam"], g["bet"], g["bq_c"], g["minus_half"], g["eps_c"])
    wq, wk, wv, wo, bq, bk, bv = g["wq"], g["wk"], g["wv"], g["wo"], g["bq"], g["bk"], g["bv"]
    k_dram, v_dram, ctx_rows = g["k_dram"], g["v_dram"], g["ctx_rows"]
    c_s = g["x_s"]

    with ExitStack() as st:
        wk_s = sb(st, "wk_s", [P, 2, DC, H], F32R)
        wv_s = sb(st, "wv_s", [P, 2, DC, H], F32R)
        w_raw = sb(st, "w_raw", [P, 2, H])
        c_n = sb(st, "c_n", [P, RT, D])
        c_T = sb(st, "c_T", [P, 2, DC, P])
        k_st = sb(st, "k_st", [P, 2, GROUP])
        v_st = sb(st, "v_st", [P, 2, H])
        bv_b = sb(st, "bv_b", [P, H])
        bk_c = sb(st, "bk_c", [P, PAIRS])
        bk_8 = sb(st, "bk_8", [P, PAIRS])
        stats = sb(st, "c_stats", [P, RT, 6])
        mv = sb(st, "c_mv", [P, RT, 2])
        counts = sb(st, "c_counts", [P, 1])
        var_eps = sb(st, "c_var_eps", [P, RT])
        rstd = sb(st, "c_rstd", [P, RT])
        ps_k = [banks[0], banks[1]]
        ps_v = [[banks[2], banks[3]], [banks[4], banks[5]]]
        ps_t = [banks[6], banks[7]]

        consts_loaded = sem("consts_loaded")
        bv_loaded = sem("bv_loaded")
        ctx_loaded = [sem(f"ctx_loaded{t}") for t in range(RT)]
        consts_made = sem("consts_made")
        w_rounded_v = sem("w_rounded_v")
        w_rounded_a = sem("w_rounded_a")
        w_split_v = sem("w_split_v")
        w_split_g = sem("w_split_g")
        bk_scaled = sem("bk_scaled")
        c_stats_done = sem("c_stats_done")
        c_aggregated = sem("c_aggregated")
        c_var_eps = sem("c_var_eps")
        c_counted = sem("c_counted")
        c_rstd_done = sem("c_rstd_done")
        c_normed = sem("c_normed")
        c_transposed = sem("c_transposed")
        cT_ready = sem("cT_ready")
        c_rounded = sem("c_rounded")
        c_split = sem("c_split")
        k_projected = sem("k_projected")
        k_ready = sem("k_ready")
        k_stored = [sem("k_stored0"), sem("k_stored1")]
        v_projected = sem("v_projected")
        v_ready = sem("v_ready")
        v_stored = [sem("v_stored0"), sem("v_stored1")]

        chunks = [(w.rearrange("(c p) n -> c p n", p=P)[c], [ws[:, i, c, :] for i in range(2)])
                  for w, ws in ((wv, wv_s), (wk, wk_s), (wq, wq_s)) for c in range(DC)]
        chunks += [(wo.rearrange("(c a p) n -> c p a n", p=P, a=2)[c],
                    [wo_s[:, i, 2 * c:2 * c + 2, :] for i in range(2)]) for c in range(PAIRS // 2)]
        staging = [w_raw[:, i, :] for i in range(2)]
        staging += [buf[:, 2 * i:2 * i + 2, :].rearrange("p t d -> p (t d)") for buf in (g["x_in"], g["x_n"]) for i in range(2)]
        SLOTS = len(staging)
        w_loaded = [sem(f"w_loaded{n}") for n in range(SLOTS)]

        EARLY = 2 * DC
        ROUND_ACT = [0, 1] + list(range(DC, EARLY))
        SPLIT_POOL = [1, 3, DC + 1, DC + 3]

        def rounded(n):
            on_act = n in ROUND_ACT
            return (w_rounded_a if on_act else w_rounded_v), sum((m in ROUND_ACT) == on_act for m in range(n + 1))

        def split(n):
            on_pool = n in SPLIT_POOL
            return (w_split_g if on_pool else w_split_v), sum((m in SPLIT_POOL) == on_pool for m in range(n + 1))

        def raw(n):
            staged = staging[n % SLOTS]
            return staged if n < 3 * DC else staged.rearrange("p (a n) -> p a n", a=2)

        block = st.enter_context(nc.Block())

        @block.sync
        def _(sp):
            def load_context(row, t):
                sp.dma_start(c_n[:, t, :], ctx_rows[bass.ds(row, P), :]).then_inc(ctx_loaded[t], 16)

            def load_weight(n):
                if n >= SLOTS:
                    sp.wait_ge(*split(n - SLOTS))
                sp.dma_start(raw(n), chunks[n][0]).then_inc(w_loaded[n % SLOTS], 16)

            load_context(0, 0)
            for dst, src in ((gam, g["gamma"]), (bet, g["beta"]), (bq_c, bq), (bk_c, bk)):
                sp.dma_start(dst[:, :], src).then_inc(consts_loaded, 16)
            for t in range(1, RT):
                load_context(t * P, t)
            for n in range(EARLY):
                load_weight(n)
            sp.dma_start(bv_b[:, :], bv.rearrange("(a n) -> a n", a=1).to_broadcast([P, H])).then_inc(bv_loaded, 16)

            def group(r, first, last):
                if not last:
                    next_rows = [offset(sp, r * STEP + STEP + t * P) for t in range(RT)]
                    for t in range(RT):
                        sp.wait_ge(c_transposed, RT * r + t + 1)
                        load_context(next_rows[t], t)
                if first:
                    for n in range(EARLY, len(chunks)):
                        load_weight(n)

            group(0, True, False)
            with sp.Fori(1, GROUPS - 1) as r:
                group(r, False, False)
            sp.wait_ge(w_split_v, len(chunks) - len(SPLIT_POOL))
            sp.dma_start(g["x_in"][:, :, :], g["x"].rearrange("b s d -> (b s) d")[0:g["S"], :].rearrange("(t p) d -> p t d", p=P)).then_inc(g["x_loaded"], 16)
            for s in range(2):
                sp.wait_ge(k_stored[s], 16 * (PAIRS // 2))
            load_keys(sp, g, 0)
            for s in range(2):
                sp.wait_ge(k_stored[s], 16 * (PAIRS // 2) * GROUPS)
                sp.wait_ge(v_stored[s], 16 * (RT // 2) * GROUPS)

        @block.gpsimd
        def _(pool):
            pool.memset(ident[:, :], 0.0).then_inc(consts_made, 1)
            pool.memset(minus_half[:, :], -0.5).then_inc(consts_made, 1)
            pool.memset(eps_c[:, :], EPS).then_inc(consts_made, 1)
            pool.wait_ge(consts_made, 3)
            pool.affine_select(out=ident[:, :], in_=ident[:, :], compare_op=ALU.not_equal, fill=1.0, base=0,
                               pattern=[[-1, P]], channel_multiplier=1).then_inc(consts_made, 1)

            def rstd_of(r):
                pool.wait_ge(c_aggregated, RT * (r + 1))
                pool.tensor_tensor(var_eps[:, :], mv[:, :, 1], eps_c[:, 0:RT], ALU.add).then_inc(c_var_eps, 1)
                pool.wait_ge(c_var_eps, r + 1)
                pool.tensor_tensor(rstd[:, :], var_eps[:, :], minus_half[:, 0:RT], ALU.pow).then_inc(c_rstd_done, 1)

            rstd_of(0)
            for n in SPLIT_POOL:
                hi, lo = chunks[n][1]
                pool.wait_ge(*rounded(n))
                pool.tensor_tensor(lo, raw(n), hi.bitcast(F32), ALU.subtract).then_inc(w_split_g, 1)
            with pool.Fori(1, GROUPS) as r:
                rstd_of(r)
            x_inverse_deviation(pool, g, 0)
            x_low(pool, g, 0, range(DC // 2), g["x_split_g"])

        @block.vector
        def _(dve):
            def statistics(r):
                for t in range(RT):
                    dve.wait_ge(ctx_loaded[t], 16 * (r + 1))
                    nc.vector.bn_stats(stats[:, t, :], c_n[:, t, :]).then_inc(c_stats_done, 1)
                dve.wait_ge(c_stats_done, RT * (r + 1))
                nc.vector.tensor_copy(counts[:, :], stats[:, RT - 1, 0:1]).then_inc(c_counted, 1)
                for t in range(RT):
                    nc.vector.bn_aggr(mv[:, t, :], stats[:, t, :]).then_inc(c_aggregated, 1)

            def normalise(r):
                for t in range(RT):
                    dve.wait_ge(c_rstd_done, r + 1)
                    nc.vector.tensor_scalar(c_n[:, t, :], c_n[:, t, :], mv[:, t, 0:1], rstd[:, t:t + 1],
                                            ALU.subtract, ALU.mult).then_inc(c_normed, 1)

            def round_weight(n):
                dve.wait_ge(w_loaded[n % SLOTS], 16 * (n // SLOTS + 1))
                nc.vector.tensor_copy(chunks[n][1][0], raw(n)).then_inc(w_rounded_v, 1)

            def weight_low(n):
                hi, lo = chunks[n][1]
                dve.wait_ge(*rounded(n))
                nc.vector.tensor_tensor(lo, raw(n), hi.bitcast(F32), ALU.subtract).then_inc(w_split_v, 1)

            def split_context(r, t):
                cols = slice(t * P, (t + 1) * P)
                dve.wait_ge(cT_ready, (RT * r + t + 1) * DC)
                nc.vector.tensor_copy(c_s[:, 0, :, cols], c_T[:, t % 2]).then_inc(c_rounded, 1)
                dve.wait_ge(c_rounded, RT * r + t + 1)
                nc.vector.tensor_tensor(c_s[:, 1, :, cols], c_T[:, t % 2], c_s[:, 0, :, cols].bitcast(F32),
                                        ALU.subtract).then_inc(c_split, 1)

            dve.wait_ge(consts_loaded, 64)
            nc.vector.tensor_scalar(bk_8[:, :], bk_c[:, :], K_SCALE, None, ALU.mult).then_inc(bk_scaled, 1)
            statistics(0)
            normalise(0)
            weight_low(0)
            round_weight(3)
            round_weight(2)
            split_context(0, 0)
            weight_low(2)
            for t in range(1, RT):
                split_context(0, t)
            for n in range(DC, EARLY, 2):
                weight_low(n)
            dve.wait_ge(bv_loaded, 16)

            def add_bias(r, t, first):
                for n in range(2):
                    dve.wait_ge(v_projected, 2 * RT * r + 2 * t + n + 1)
                    if t >= 2:
                        dve.wait_ge(v_stored[t % 2], 16 * ((RT // 2) * r + 1))
                    elif not first:
                        dve.wait_ge(v_stored[t % 2], 16 * (RT // 2) * r)
                    nc.vector.tensor_tensor(v_st[:, t % 2, n * HALF:(n + 1) * HALF], ps_v[t % 2][n][:, :],
                                            bv_b[:, n * HALF:(n + 1) * HALF], ALU.add).then_inc(v_ready, 1)

            def group(r, first, last):
                add_bias(r, 0, first)
                if not last:
                    statistics(r + 1)
                    normalise(r + 1)
                else:
                    x_statistics(nc, dve, g, 0, range(RT))
                    x_aggregate(nc, dve, g, 0)
                    x_normalise(nc, dve, g, 0)
                if first:
                    for m in range(PAIRS):
                        round_weight(EARLY + m)
                        weight_low(EARLY + m)
                for t in range(RT):
                    if not last:
                        if t == 0:
                            dve.wait_ge(k_projected, PAIRS * (r + 1))
                        split_context(r + 1, t)
                    elif t < 2:
                        for c in (2 * t, 2 * t + 1):
                            dve.wait_ge(g["x_transposed"], c + 1)
                            nc.vector.tensor_scalar(g["x_in"][:, c, :], ps_t[c % 2][:, :], gam[:, c:c + 1], bet[:, c:c + 1],
                                                    ALU.mult, ALU.add).then_inc(g["xT_ready"], 1)
                    if t < RT - 1:
                        add_bias(r, t + 1, first)

            group(0, True, False)
            with dve.Fori(1, GROUPS - 1) as r:
                group(r, False, False)
            group(GROUPS - 1, False, True)
            dve.wait_ge(v_projected, 2 * RT * GROUPS)
            x_round(nc, dve, g, 0, range(DC))
            x_low(dve, g, 0, range(DC // 2, DC), g["x_split_v"])

        @block.scalar
        def _(act):
            def evacuate_transposed(r, t):
                act.wait_ge(c_transposed, RT * r + t + 1)
                if t >= 2 or type(r) is not int or r > 0:
                    act.wait_ge(c_split, RT * r + t - 1)
                for c in range(DC):
                    nc.scalar.activation(c_T[:, t % 2, c, :], ps_t[t % 2][:, c * P:(c + 1) * P], ACT.Identity,
                                         bias=bet[:, c:c + 1], scale=gam[:, c:c + 1]).then_inc(cT_ready, 1)

            def store_values(r, rows, t):
                act.wait_ge(v_ready, 2 * RT * r + 2 * t + 2)
                act.dma_start(v_dram[bass.ds(rows[t], P), :], v_st[:, t % 2, :]).then_inc(v_stored[t % 2], 16)

            def round_weight(n):
                act.wait_ge(w_loaded[n % SLOTS], 16 * (n // SLOTS + 1))
                nc.scalar.activation(chunks[n][1][0], raw(n), ACT.Copy).then_inc(w_rounded_a, 1)

            round_weight(0)
            round_weight(1)
            act.wait_ge(consts_loaded, 64)
            act.wait_ge(bk_scaled, 1)
            for t in range(RT):
                evacuate_transposed(0, t)
            for n in range(DC, EARLY):
                round_weight(n)

            def group(r, first, last):
                rows = [offset(act, r * STEP + t * P) for t in range(RT)]
                if not first:
                    act.wait_ge(v_stored[1], 16 * (RT // 2) * r)
                store_values(r, rows, 0)
                for m in range(PAIRS):
                    act.wait_ge(k_projected, PAIRS * r + m + 1)
                    if m >= 2:
                        act.wait_ge(k_stored[m % 2], 16 * ((PAIRS // 2) * r + m // 2))
                    elif not first:
                        act.wait_ge(k_stored[m % 2], 16 * (PAIRS // 2) * r)
                    nc.scalar.activation(k_st[:, m % 2, :], ps_k[m % 2][:, :], ACT.Identity,
                                         bias=bk_8[:, m:m + 1], scale=K_SCALE).then_inc(k_ready, 1)
                    act.wait_ge(k_ready, PAIRS * r + m + 1)
                    act.dma_start(k_dram[m, :, bass.ds(rows[0], GROUP)], k_st[:, m % 2, :]).then_inc(k_stored[m % 2], 16)
                for t in range(RT):
                    if not last:
                        evacuate_transposed(r + 1, t)
                    if t < RT - 1:
                        store_values(r, rows, t + 1)

            group(0, True, False)
            with act.Fori(1, GROUPS - 1) as r:
                group(r, False, False)
            group(GROUPS - 1, False, True)

        @block.tensor
        def _(pe):
            def transpose_tile(r, t, start):
                pe.wait_ge(c_normed, RT * r + t + 1)
                if not (start and t < 2):
                    pe.wait_ge(cT_ready, DC * (RT * r + t - 1))
                for c in range(DC):
                    last = nc.tensor.transpose(ps_t[t % 2][:, c * P:(c + 1) * P], c_n[:, t, c * P:(c + 1) * P],
                                               ident[:, :])
                last.then_inc(c_transposed, 1)

            def project_keys(r, first):
                pe.wait_ge(c_split, RT * (r + 1))
                for m in range(PAIRS):
                    if m >= 2 or not first:
                        pe.wait_ge(k_ready, PAIRS * r + m - 1)
                    cols = slice(m * P, (m + 1) * P)
                    for c in range(DC):
                        if first and m == 0:
                            pe.wait_ge(*split(DC + c))
                        mm = three_passes(nc, ps_k[m % 2][:, :], (wk_s[:, 0, c, cols], wk_s[:, 1, c, cols]),
                                          (c_s[:, 0, c, :], c_s[:, 1, c, :]), c == 0, c == DC - 1)
                    mm.then_inc(k_projected, 1)

            def project_values(r, t, first):
                rows = slice(t * P, (t + 1) * P)
                for n in range(2):
                    cols = slice(n * HALF, (n + 1) * HALF)
                    if t >= 2 or not first:
                        pe.wait_ge(v_ready, 2 * RT * r + 2 * t + n - 3)
                    if t == 0:
                        pe.wait_ge(c_split, RT * r + 1)
                    for c in range(DC):
                        if first and t == 0 and n == 0:
                            pe.wait_ge(*split(c))
                        mm = three_passes(nc, ps_v[t % 2][n][:, :], (c_s[:, 0, c, rows], c_s[:, 1, c, rows]),
                                          (wv_s[:, 0, c, cols], wv_s[:, 1, c, cols]), c == 0, c == DC - 1)
                    mm.then_inc(v_projected, 1)

            def transpose_x(c):
                pe.wait_ge(g["x_normed"], g["QT"])
                if c >= 2:
                    pe.wait_ge(g["xT_ready"], c - 1)
                for q in range(g["QT"]):
                    mm = nc.tensor.transpose(ps_t[c % 2][:, q * P:(q + 1) * P],
                                             g["x_n"][:, q, c * P:(c + 1) * P], ident[:, :])
                mm.then_inc(g["x_transposed"], 1)

            pe.wait_ge(consts_made, 4)
            for t in range(RT):
                transpose_tile(0, t, True)

            def group(r, first, last):
                project_values(r, 0, first)
                project_keys(r, first)
                for t in range(RT):
                    if last and t < 2:
                        transpose_x(2 * t)
                        transpose_x(2 * t + 1)
                    elif not last:
                        transpose_tile(r + 1, t, False)
                    if t < RT - 1:
                        project_values(r, t + 1, first)

            group(0, True, False)
            with pe.Fori(1, GROUPS - 1) as r:
                group(r, False, False)
            group(GROUPS - 1, False, True)
            pe.wait_ge(k_ready, PAIRS * GROUPS - 1)
            project_first_queries(nc, pe, g, banks[0], 0)


def attend(nc, sem, sb, banks, g):
    B, S, D, KEYS = g["B"], g["S"], g["D"], g["KEYS"]
    DH, PAIRS, DC, QT, W2 = g["DH"], g["PAIRS"], g["DC"], g["QT"], g["W2"]
    wq_s, wo_s, ident, gam, bet, bq_c = g["wq_s"], g["wo_s"], g["ident"], g["gam"], g["bet"], g["bq_c"]
    x, bo, out, k_dram, v_dram = g["x"], g["bo"], g["out"], g["k_dram"], g["v_dram"]
    x_in, x_n, k_in, k_loaded = g["x_in"], g["x_n"], g["k_in"], g["k_loaded"]
    x_loaded, x_normed, x_transposed, xT_ready = g["x_loaded"], g["x_normed"], g["x_transposed"], g["xT_ready"]
    x_s, x_rounded, x_split_v, x_split_g, q_projected = (
        g["x_s"], g["x_rounded"], g["x_split_v"], g["x_split_g"], g["q_projected"])

    x_rows = x.rearrange("b s d -> (b s) d")
    out_rows = out.rearrange("b s d -> (b s) d")
    KEYS_EARLY = 2
    PV = 3 * DH

    with ExitStack() as st:
        x_bo = sb(st, "x_bo", [P, QT, D])
        q_s = sb(st, "q_s", [P, 2, 2, S], F32R)
        k_s = sb(st, "k_s", [P, 2, PAIRS, W2], F32R)
        v_in = sb(st, "v_in", [KEYS, PAIRS, 2, DH])
        v_s = sb(st, "v_s", [KEYS, 2, PAIRS, PV], F32R)
        prob = sb(st, "prob", [P, 2, QT, 2, KEYS])
        pT_s = sb(st, "pT_s", [KEYS, 2, 2, 2, S], F32R)
        o_s = sb(st, "o_s", [P, 2, PAIRS, S], F32R)
        o_out = sb(st, "o_out", [P, 2, D])
        bo_b = sb(st, "bo_b", [P, D])
        neg_max = sb(st, "neg_max", [P, 2, QT, 2])
        sums = sb(st, "sums", [P, 2, QT, 2])
        recip = sb(st, "recip", [P, 2, QT, 2])
        v_halves = [v_s[:, i].rearrange("k m (a d) -> k m a d", a=3)[:, :, 0:3:2, :] for i in range(2)]
        ps_proj = [banks[0], banks[1]]
        ps_s = [banks[2], banks[3]]
        ps_pT = [banks[4], banks[5]]
        ps_o = [banks[6], banks[7]]

        bo_loaded = sem("bo_loaded")
        x_reloaded = sem("x_reloaded")
        v_loaded = sem("v_loaded")
        keys_zeroed = sem("keys_zeroed")
        values_zeroed = sem("values_zeroed")
        residual_ready = sem("residual_ready")
        kb_rounded = sem("kb_rounded")
        kb_split = sem("kb_split")
        vb_rounded = sem("vb_rounded")
        vb_split = sem("vb_split")
        q_hi = sem("q_hi")
        q_lo = sem("q_lo")
        scores_ready = sem("scores_ready")
        max_ready = sem("max_ready")
        exp_ready = sem("exp_ready")
        recip_ready = sem("recip_ready")
        probs_ready = sem("probs_ready")
        probs_transposed = sem("probs_transposed")
        pT_hi = sem("pT_hi")
        pT_lo = sem("pT_lo")
        o_ready = sem("o_ready")
        o_hi = sem("o_hi")
        o_lo = sem("o_lo")
        out_projected = sem("out_projected")
        out_ready = sem("out_ready")
        out_stored = [sem("out_stored0"), sem("out_stored1")]

        Q_BANK = [0, 1, 0, 1, 1, 1, 1, 1]
        OUT_BANK = [1, 0, 1, 0]

        block = st.enter_context(nc.Block())


        @block.sync
        def _(sp):
            def load_x(row, dst, loaded):
                sp.dma_start(dst[:, :, :], x_rows[bass.ds(row, S), :].rearrange("(t p) d -> p t d", p=P)).then_inc(loaded, 16)

            def load_v(key):
                sp.dma_start(v_in[:, :, :, :], v_dram[bass.ds(key, KEYS), :].rearrange("k (m a d) -> k m a d", m=PAIRS, a=2)).then_inc(v_loaded, 16)

            def store_out(b, rows):
                for t in range(QT):
                    sp.wait_ge(out_ready, QT * b + t + 1)
                    sp.dma_start(out_rows[bass.ds(rows[t], P), :], o_out[:, t % 2, :]).then_inc(out_stored[t % 2], 16)

            def batch(b, first, last):
                if not last:
                    next_row, next_key = offset(sp, b * S + S), offset(sp, b * KEYS + KEYS)
                if not first:
                    row = offset(sp, b * S)
                    out_row = [offset(sp, b * S + (t * P - S)) for t in range(QT)]
                if not last:
                    sp.wait_ge(x_split_v, DC // 2 * (b + 1))
                    sp.wait_ge(x_split_g, DC // 2 * (b + 1))
                    load_x(next_row, x_in, x_loaded)
                    if first:
                        load_v(0)
                        sp.dma_start(bo_b[:, :], bo.rearrange("(a n) -> a n", a=1).to_broadcast([P, D])).then_inc(bo_loaded, 16)
                        load_x(0, x_bo, x_reloaded)
                    sp.wait_ge(kb_split, 4 * b + 4)
                    load_keys(sp, g, next_key)
                    sp.wait_ge(vb_split, b + 1)
                    load_v(next_key)
                if not first:
                    store_out(b - 1, out_row)
                    load_x(row, x_bo, x_reloaded)

            batch(0, True, False)
            with sp.Fori(1, B - 1) as b:
                batch(b, False, False)
            batch(B - 1, False, True)
            store_out(B - 1, [(B - 1) * S + t * P for t in range(QT)])
            for s in range(2):
                sp.wait_ge(out_stored[s], 16 * (QT // 2) * B)

        @block.gpsimd
        def _(pool):
            def residual(b, tiles):
                for t in tiles:
                    pool.wait_ge(x_reloaded, 16 * (b + 1))
                    pool.tensor_tensor(x_bo[:, t, :], x_bo[:, t, :], bo_b[:, :], ALU.add).then_inc(residual_ready, 1)

            def values_low(b):
                pool.wait_ge(vb_rounded, b + 1)
                pool.tensor_tensor(v_halves[1], v_in[:, :, :, :], v_halves[0].bitcast(F32), ALU.subtract).then_inc(vb_split, 1)

            def divide(b, p):
                for h in range(2):
                    pr = prob[:, p % 2, 2 * h:2 * h + 2].rearrange("p t a k -> p (t a) k")
                    rc = recip[:, p % 2, 2 * h:2 * h + 2].rearrange("p t a -> p (t a)")
                    pool.wait_ge(recip_ready, 2 * (PAIRS * b + p) + h + 1)
                    pool.tensor_tensor(pr, pr, rc[:, :, None].to_broadcast([P, 4, KEYS]), ALU.mult).then_inc(probs_ready, 1)

            pool.memset(k_s[:, :, :, :].bitcast(F32), 0.0).then_inc(keys_zeroed, 1)
            pool.memset(v_s[:, :, :, :].bitcast(F32), 0.0).then_inc(values_zeroed, 1)
            pool.wait_ge(bo_loaded, 16)
            pool.wait_ge(values_zeroed, 1)

            def batch(b, first, last):
                if not first:
                    divide(b - 1, 7)
                for p in range(1, PAIRS):
                    if p == 7 and not last:
                        x_low(pool, g, b + 1, range(DC // 2), x_split_g)
                    divide(b, p - 1)
                    if p == 1 and first:
                        x_inverse_deviation(pool, g, b + 1)
                    if p == 2 and first:
                        values_low(b)
                    if p == 2 and not first:
                        residual(b - 1, [0, 1])
                        values_low(b)
                        if not last:
                            x_inverse_deviation(pool, g, b + 1)
                        residual(b - 1, [2, 3])

            batch(0, True, False)
            with pool.Fori(1, B - 1) as b:
                batch(b, False, False)
            batch(B - 1, False, True)
            divide(B - 1, 7)
            residual(B - 1, range(QT))

        @block.vector
        def _(dve):
            def statistics(b, tiles=range(QT)):
                x_statistics(nc, dve, g, b, tiles)

            def aggregate(b):
                x_aggregate(nc, dve, g, b)

            def normalise_x(b):
                x_normalise(nc, dve, g, b)

            def values_high(b, first):
                dve.wait_ge(v_loaded, 16 * (b + 1))
                if not first:
                    dve.wait_ge(o_ready, PAIRS * b)
                nc.vector.tensor_copy(v_halves[0], v_in[:, :, :, :]).then_inc(vb_rounded, 1)

            def shift_x(b, c):
                dve.wait_ge(x_transposed, DC * b + c + 1)
                nc.vector.tensor_scalar(x_in[:, c, :], ps_proj[0][:, :], gam[:, c:c + 1], bet[:, c:c + 1],
                                        ALU.mult, ALU.add).then_inc(xT_ready, 1)

            def split_keys(b, part, used):
                pairs = slice(0, KEYS_EARLY) if part == 0 else slice(KEYS_EARLY, PAIRS)
                for a in range(2):
                    rows, cols = slice(a * DH, (a + 1) * DH), slice(a * KEYS, (a + 1) * KEYS)
                    dve.wait_ge(k_loaded, 16 * (b + 1))
                    if used is not None:
                        dve.wait_ge(scores_ready, used)
                    nc.vector.tensor_copy(k_s[rows, 0, pairs, cols], k_in[rows, pairs]).then_inc(kb_rounded, 1)
                for a in range(2):
                    rows, cols = slice(a * DH, (a + 1) * DH), slice(a * KEYS, (a + 1) * KEYS)
                    dve.wait_ge(kb_rounded, 4 * b + 2 * part + a + 1)
                    nc.vector.tensor_tensor(k_s[rows, 1, pairs, cols], k_in[rows, pairs],
                                            k_s[rows, 0, pairs, cols].bitcast(F32), ALU.subtract).then_inc(kb_split, 1)

            def query_low(b, p):
                j = PAIRS * b + p
                dve.wait_ge(q_hi, j + 1)
                nc.vector.scalar_tensor_tensor(out=q_s[:, p % 2, 1, :], in0=ps_proj[Q_BANK[p]][:, :],
                                               scalar=bq_c[:, p:p + 1], in1=q_s[:, p % 2, 0, :].bitcast(F32),
                                               op0=ALU.add, op1=ALU.subtract).then_inc(q_lo, 1)

            def maxima(b, p, halves):
                for h in halves:
                    dve.wait_ge(scores_ready, 2 * (PAIRS * b + p) + h + 1)
                    nc.vector.tensor_reduce(neg_max[:, p % 2, 2 * h:2 * h + 2, :].rearrange("p t a -> p (t a)"),
                                            ps_s[h][:, 0:2 * W2].rearrange("p (t k) -> p t k", k=KEYS),
                                            AX_X, ALU.max, negate=True).then_inc(max_ready, 1)

            def reciprocals(b, p):
                for h in range(2):
                    dve.wait_ge(exp_ready, 2 * (PAIRS * b + p) + h + 1)
                    nc.vector.reciprocal(recip[:, p % 2, 2 * h:2 * h + 2, :], sums[:, p % 2, 2 * h:2 * h + 2, :]).then_inc(recip_ready, 1)

            def probs_low(b, p):
                for a in range(2):
                    dve.wait_ge(pT_hi, 2 * (PAIRS * b + p) + a + 1)
                    nc.vector.tensor_tensor(pT_s[:, p % 2, a, 1, :], ps_pT[a][0:KEYS, :],
                                            pT_s[:, p % 2, a, 0, :].bitcast(F32), ALU.subtract).then_inc(pT_lo, 1)

            def output_low(b, p):
                dve.wait_ge(o_hi, PAIRS * b + p + 1)
                nc.vector.tensor_tensor(o_s[:, 1, p, :], ps_o[p % 2][:, :], o_s[:, 0, p, :].bitcast(F32),
                                        ALU.subtract).then_inc(o_lo, 1)

            def add_residual(b, tiles):
                for t in tiles:
                    dve.wait_ge(out_projected, QT * b + t + 1)
                    dve.wait_ge(residual_ready, QT * b + t + 1)
                    if t >= 2:
                        dve.wait_ge(out_stored[t % 2], 16 * ((QT // 2) * b + 1))
                    nc.vector.tensor_tensor(o_out[:, t % 2, :], ps_proj[OUT_BANK[t]][:, :], x_bo[:, t, :],
                                            ALU.add).then_inc(out_ready, 1)

            dve.wait_ge(keys_zeroed, 1)
            split_keys(0, 0, None)

            def batch(b, first, last):
                for p in range(PAIRS):
                    one, two, three = (None if first and p < lag else (b - (p < lag), (p - lag) % PAIRS) for lag in (1, 2, 3))
                    if p == 6 and not first:
                        for s in range(2):
                            dve.wait_ge(out_stored[s], 16 * (QT // 2) * b)
                    if one:
                        maxima(*one, [0])
                    if p < 7:
                        query_low(b, p)
                    elif not last:
                        x_low(dve, g, b + 1, [3], x_split_v)
                    if p == 2 and not first:
                        output_low(*three)
                    if one:
                        maxima(*one, [1])
                    if p == 1 and first:
                        statistics(b + 1, range(0, 2))
                    if p == 2 and first:
                        dve.wait_ge(values_zeroed, 1)
                        values_high(b, first)
                    if p == 7:
                        query_low(b, 7)
                    if 3 <= p < 3 + DC and not last:
                        shift_x(b + 1, p - 3)
                    if p == 0 and first:
                        split_keys(b, 1, None)
                    if p == 3 and not last:
                        split_keys(b + 1, 0, 2 * (PAIRS * b + KEYS_EARLY))
                    if one:
                        reciprocals(*one)
                    if p == 1 and first:
                        statistics(b + 1, range(2, QT))
                        aggregate(b + 1)
                    if p == 2 and first:
                        normalise_x(b + 1)
                    if two:
                        probs_low(*two)
                    if p == 6 and not last:
                        dve.wait_ge(q_projected, PAIRS * (b + 1))
                        x_round(nc, dve, g, b + 1, range(DC))
                        x_low(dve, g, b + 1, [2], x_split_v)
                    if p != 2 and three:
                        output_low(*three)
                    if p == 2 and not first:
                        split_keys(b, 1, 2 * PAIRS * b)
                        values_high(b, first)
                        if not last:
                            statistics(b + 1)
                            aggregate(b + 1)
                        add_residual(b - 1, [0])
                        if not last:
                            normalise_x(b + 1)
                        add_residual(b - 1, range(1, QT))

            batch(0, True, False)
            with dve.Fori(1, B - 1) as b:
                batch(b, False, False)
            batch(B - 1, False, True)
            maxima(B - 1, 7, range(2))
            reciprocals(B - 1, 7)
            probs_low(B - 1, 6)
            output_low(B - 1, 5)
            probs_low(B - 1, 7)
            output_low(B - 1, 6)
            output_low(B - 1, 7)
            add_residual(B - 1, range(QT))

        @block.scalar
        def _(act):
            def query_high(b, p, first):
                j = PAIRS * b + p
                act.wait_ge(q_projected, j + 1)
                if not (first and p < 2):
                    act.wait_ge(scores_ready, 2 * j - 2)
                nc.scalar.activation(q_s[:, p % 2, 0, :], ps_proj[Q_BANK[p]][:, :], ACT.Identity,
                                     bias=bq_c[:, p:p + 1]).then_inc(q_hi, 1)

            def exponentials(b, p, first):
                j = PAIRS * b + p
                if not (first and p < 2):
                    act.wait_ge(probs_transposed, 2 * j - 2)
                for h in range(2):
                    act.wait_ge(max_ready, 2 * j + h + 1)
                    for n in range(4):
                        t, a = 2 * h + n // 2, n % 2
                        last = nc.scalar.activation(prob[:, p % 2, t, a, :], ps_s[h][:, n * KEYS:(n + 1) * KEYS], ACT.Exp,
                                                    bias=neg_max[:, p % 2, t, a:a + 1],
                                                    accum_out=sums[:, p % 2, t, a:a + 1])
                    last.then_inc(exp_ready, 1)

            def probs_high(b, p, first):
                j = PAIRS * b + p
                for a in range(2):
                    act.wait_ge(probs_transposed, 2 * j + a + 1)
                    if not (first and p < 2):
                        act.wait_ge(o_ready, j - 1)
                    nc.scalar.activation(pT_s[:, p % 2, a, 0, :], ps_pT[a][0:KEYS, :], ACT.Copy).then_inc(pT_hi, 1)

            def output_high(b, p, first):
                act.wait_ge(o_ready, PAIRS * b + p + 1)
                if p == 0 and not first:
                    act.wait_ge(out_projected, QT * b)
                nc.scalar.activation(o_s[:, 0, p, :], ps_o[p % 2][:, :], ACT.Copy).then_inc(o_hi, 1)

            def batch(b, first):
                for p in range(PAIRS):
                    one, two, three = (None if first and p < lag else (b - (p < lag), (p - lag) % PAIRS) for lag in (1, 2, 3))
                    if p < 7:
                        query_high(b, p, first)
                    if p == 2 and not first:
                        output_high(*three, first)
                    if one:
                        exponentials(*one, first)
                    if two:
                        probs_high(*two, first)
                    if p == 6:
                        query_high(b, 7, first)
                    if p != 2 and three:
                        output_high(*three, first)

            batch(0, True)
            with act.Fori(1, B) as b:
                batch(b, False)
            exponentials(B - 1, 7, False)
            probs_high(B - 1, 6, False)
            output_high(B - 1, 5, False)
            probs_high(B - 1, 7, False)
            output_high(B - 1, 6, False)
            output_high(B - 1, 7, False)

        @block.tensor
        def _(pe):
            def transpose_x(b, c, first):
                if c == 0:
                    pe.wait_ge(x_normed, QT * (b + 1))
                    if first:
                        pe.wait_ge(q_lo, 3)
                    else:
                        pe.wait_ge(out_ready, QT * (b - 1))
                else:
                    pe.wait_ge(xT_ready, DC * b + c)
                for t in range(QT):
                    last = nc.tensor.transpose(ps_proj[0][:, t * P:(t + 1) * P],
                                               x_n[:, t, c * P:(c + 1) * P], ident[:, :])
                last.then_inc(x_transposed, 1)

            def project_queries(b, p, first):
                if p == 0:
                    pe.wait_ge(xT_ready, DC * (b + 1))
                    return project_first_queries(nc, pe, g, ps_proj[0], b)
                if p == 1 and not first:
                    pe.wait_ge(q_lo, PAIRS * b)
                elif p == 2:
                    pe.wait_ge(q_lo, PAIRS * b + 1)
                elif p == 3 and first:
                    pe.wait_ge(q_lo, PAIRS * b + 2)
                elif p == 3:
                    pe.wait_ge(out_ready, QT * (b - 1) + 3)
                elif p > 3:
                    pe.wait_ge(q_lo, PAIRS * b + p)
                cols = slice(p * P, (p + 1) * P)
                for c in range(DC):
                    mm = three_passes(nc, ps_proj[Q_BANK[p]][:, :], (wq_s[:, 0, c, cols], wq_s[:, 1, c, cols]),
                                      (x_s[:, 0, c, :], x_s[:, 1, c, :]), c == 0, c == DC - 1)
                mm.then_inc(q_projected, 1)

            def score(b, p, n, first):
                j = PAIRS * b + p
                t, way = n // 3, n % 3
                h = t // 2
                if n == 0:
                    pe.wait_ge(q_lo, j + 1)
                    if p == 0:
                        pe.wait_ge(kb_split, 4 * b + 2)
                    if p == KEYS_EARLY:
                        pe.wait_ge(kb_split, 4 * b + 4)
                if n % 6 == 0 and not (first and p == 0):
                    pe.wait_ge(exp_ready, 2 * j + h - 1)
                q_part, k_part = ((0, 0), (0, 1), (1, 0))[way]
                mm = nc.tensor.matmul(ps_s[h][:, (t % 2) * W2:(t % 2 + 1) * W2], q_s[:, p % 2, q_part, t * P:(t + 1) * P],
                                      k_s[:, k_part, p, :], start=way == 0, stop=way == 2)
                if n % 6 == 5:
                    mm.then_inc(scores_ready, 1)

            def transpose_prob(b, p, n, first):
                j = PAIRS * b + p
                a, t = n // QT, n % QT
                if n == 0:
                    pe.wait_ge(probs_ready, 2 * j + 2)
                if t == 0 and not (first and p == 0):
                    pe.wait_ge(pT_lo, 2 * j + a - 1)
                mm = nc.tensor.transpose(ps_pT[a][0:KEYS, t * P:(t + 1) * P], prob[:, p % 2, t, a, :], ident[:, :])
                if t == QT - 1:
                    mm.then_inc(probs_transposed, 1)

            def scores(b, p, first):
                for n in range(3 * QT):
                    score(b, p, n, first)

            def transpose_probs(b, p, first):
                for n in range(2 * QT):
                    transpose_prob(b, p, n, first)

            def scores_and_transposes(b, p, b2, p2, first):
                ahead = QT
                for n in range(3 * QT):
                    score(b, p, n, first)
                    if n >= ahead:
                        transpose_prob(b2, p2, n - ahead, first)

            def weigh_values(b, p, first):
                j = PAIRS * b + p
                if not (first and p < 2):
                    pe.wait_ge(o_lo, j - 1)
                if p == 0:
                    pe.wait_ge(vb_split, b + 1)
                for a in range(2):
                    pe.wait_ge(pT_lo, 2 * j + a + 1)
                    cols = slice(a * DH, a * DH + P)
                    mm = three_passes(nc, ps_o[p % 2][:, :], (v_s[:, 0, p, cols], v_s[:, 1, p, cols]),
                                      (pT_s[:, p % 2, a, 0, :], pT_s[:, p % 2, a, 1, :]), a == 0, a == 1)
                mm.then_inc(o_ready, 1)

            def output_tile(b, t, pairs, at_end):
                rows = slice(t * P, (t + 1) * P)
                for p in pairs:
                    if p == 0 and at_end:
                        if t == 0:
                            pe.wait_ge(q_lo, PAIRS * (b + 1))
                    elif p == 0 and t < 2:
                        pe.wait_ge(q_lo, PAIRS * (b + 1) + 2 + t)
                    if p == 0 and t >= 2:
                        pe.wait_ge(out_ready, QT * b + t - 1)
                    if t == 0 and at_end:
                        pe.wait_ge(o_lo, PAIRS * b + p + 1)
                    elif t == 0 and p in (0, PAIRS - 1):
                        pe.wait_ge(o_lo, PAIRS * (b + 1) - (p == 0))
                    mm = three_passes(nc, ps_proj[OUT_BANK[t]][:, :], (o_s[:, 0, p, rows], o_s[:, 1, p, rows]),
                                      (wo_s[:, 0, p, :], wo_s[:, 1, p, :]), p == 0, p == PAIRS - 1)
                if p == PAIRS - 1:
                    mm.then_inc(out_projected, 1)

            def batch(b, first, last):
                for p in range(PAIRS):
                    one, two, three = (None if first and p < lag else (b - (p < lag), (p - lag) % PAIRS) for lag in (1, 2, 3))
                    if p < 7 and not (first and p == 0):
                        project_queries(b, p, first)
                    if p == 2 and not first:
                        weigh_values(*three, first)
                    if two:
                        scores_and_transposes(*one, *two, first)
                    elif one:
                        scores(*one, first)
                    if 3 <= p < 3 + DC and not last:
                        transpose_x(b + 1, p - 3, first)
                    if p == 6:
                        project_queries(b, 7, first)
                    if p != 2 and three:
                        weigh_values(*three, first)
                    if p == 2 and not first:
                        for t in range(QT):
                            output_tile(b - 1, t, range(PAIRS), False)

            batch(0, True, False)
            with pe.Fori(1, B - 1) as b:
                batch(b, False, False)
            batch(B - 1, False, True)
            scores(B - 1, 7, False)
            weigh_values(B - 1, 5, False)
            output_tile(B - 1, 0, range(0, 2), True)
            transpose_probs(B - 1, 6, False)
            output_tile(B - 1, 0, range(2, 5), True)
            transpose_probs(B - 1, 7, False)
            weigh_values(B - 1, 6, False)
            output_tile(B - 1, 0, range(5, 6), True)
            weigh_values(B - 1, 7, False)
            output_tile(B - 1, 1, range(0, 6), True)
            for t in range(2):
                output_tile(B - 1, t, range(6, PAIRS), True)
            for t in range(2, QT):
                output_tile(B - 1, t, range(PAIRS), True)


def kernel(**inputs):
    import numpy as np
    import concourse.bacc as bacc
    from concourse.bass_utils import run_bass_kernel_spmd

    def columns(a):
        return np.ascontiguousarray(np.asarray(a).reshape(-1, P).T)

    layer = "L0_xattn_"
    arrays = {
        "x": inputs["x"], "ctx": inputs["ctx_1024"],
        "wq": inputs[layer + "Wq"], "bq": columns(inputs[layer + "bq"]),
        "wk": inputs[layer + "Wk"], "bk": columns(inputs[layer + "bk"]),
        "wv": inputs[layer + "Wv"], "bv": inputs[layer + "bv"],
        "wo": inputs[layer + "Wo"], "bo": inputs[layer + "bo"],
        "gamma": columns(inputs[layer + "ln_gamma"]), "beta": columns(inputs[layer + "ln_beta"]),
    }
    arrays = {f"in_{n}": np.ascontiguousarray(a) for n, a in arrays.items()}
    nc = bacc.Bacc("TRN2", target_bir_lowering=False, num_devices=1)
    args = [nc.dram_tensor(n, a.shape, mybir.dt.from_np(a.dtype), kind="ExternalInput").ap() for n, a in arrays.items()]
    out = nc.dram_tensor("out", inputs["x"].shape, F32, kind="ExternalOutput").ap()
    build_kernel(nc, *args, out)
    result = run_bass_kernel_spmd(nc, [arrays], core_ids=[0])
    return result.results[0]["out"]
```
